# Optimizing a Trainium2 kernel written in Bass

```python
import numpy as np
import jax
import jax.numpy as jnp

def _softmax(x, axis=-1):
    return jax.nn.softmax(x, axis=axis)

def _gelu(x):
    return jax.nn.gelu(x, approximate=True)

def _silu(x):
    return jax.nn.silu(x)

def _sigmoid(x):
    return jax.nn.sigmoid(x)

def _layernorm(x, axis=-1, eps=1e-05):
    m = jnp.mean(x, axis=axis, keepdims=True)
    v = jnp.var(x, axis=axis, keepdims=True)
    return (x - m) / jnp.sqrt(v + eps)

def _scatter_add(tgt, idx, src, axis=0):
    return tgt.at[idx].add(src)

def _segment_sum(src, seg, n):
    return jax.ops.segment_sum(src, seg, n)
kernel_name = 'mk_gnn_resnorm_d4_gnn_r16_31a147'

def setup_inputs(seed: int=0):
    np.random.seed(seed)
    _w = jnp.asarray

    def _rec_inputs():
        import jax
        import jax.numpy as jnp
        _gk = jax.random.key(seed)
        x = -0.000202 + 1 * jax.random.normal(jax.random.fold_in(_gk, 1), (6250, 64), jnp.float32)
        _s = jax.random.randint(jax.random.fold_in(_gk, 2), (100000,), 0, 6250, jnp.int32)
        _d = jax.random.randint(jax.random.fold_in(_gk, 3), (100000,), 0, 6250, jnp.int32)
        _loop = jnp.arange(6250, dtype=jnp.int32)
        src = jnp.concatenate([_s, _d, _loop])
        dst = jnp.concatenate([_d, _s, _loop])
        _o = jnp.argsort(dst, stable=True)
        src = src[_o]
        dst = dst[_o]
        edge_attr_64 = -8.16379e-05 + 0.999858 * jax.random.normal(jax.random.fold_in(_gk, 12), (206250, 64), jnp.float32)
        return (x, src, dst, edge_attr_64)
    x, src, dst, edge_attr_64 = _rec_inputs()

    def _L0_gnn_setup():
        import jax, jax.numpy as jnp
        import numpy as np
        N_NODES = 6250
        N_EDGES = 100000
        D_IN = 64
        D_OUT = 64
        key = jax.random.key(seed)
        k_h, k_e, k_src, k_dst, k_w = jax.random.split(key, 5)
        h = jax.random.normal(k_h, (N_NODES, D_IN), dtype=jnp.float32)
        e = jax.random.normal(k_e, (N_EDGES, D_IN), dtype=jnp.float32)
        src = jax.random.randint(k_src, (N_EDGES,), 0, N_NODES, dtype=jnp.int32)
        dst = jax.random.randint(k_dst, (N_EDGES,), 0, N_NODES, dtype=jnp.int32)
        W = jax.random.normal(k_w, (D_OUT, 2 * D_IN), dtype=jnp.float32) * (1.0 / np.sqrt(2 * D_IN))
        b = jnp.zeros((D_OUT,), dtype=jnp.float32)
        return {'h': h, 'e': e, 'src': src, 'dst': dst, 'W': W, 'b': b}
    _L0_gnn_all = _L0_gnn_setup()
    _L0_gnn_in = {k: v for k, v in _L0_gnn_all.items() if k in ('W', 'b')}
    del _L0_gnn_all

    def _L1_gnn_setup():
        import jax, jax.numpy as jnp
        import numpy as np
        N, E, D = (3125, 50000, 64)
        EPS = 1e-05

        def _gcn_norm(edge_index, n_nodes):
            loop = jnp.arange(n_nodes, dtype=edge_index.dtype)
            src = jnp.concatenate([edge_index[0], loop])
            dst = jnp.concatenate([edge_index[1], loop])
            deg = jax.ops.segment_sum(jnp.ones_like(dst, dtype=jnp.float32), dst, num_segments=n_nodes)
            dinv = jnp.where(deg > 0, jax.lax.rsqrt(deg), 0.0)
            norm = dinv[src] * dinv[dst]
            return (src, dst, norm)

        def _layer(x, src, dst, norm, W, b, gamma, beta):
            h = x @ W
            msg = h[src] * norm[:, None]
            agg = jax.ops.segment_sum(msg, dst, num_segments=x.shape[0]) + b
            mean = jnp.mean(agg, axis=0)
            var = jnp.mean(jnp.square(agg - mean), axis=0)
            y = (agg - mean) * jax.lax.rsqrt(var + EPS) * gamma + beta
            return jax.nn.elu(y)
        key = jax.random.key(seed)
        ks = jax.random.split(key, 16)
        inp = {'x': jax.random.normal(ks[0], (N, D), dtype=jnp.float32), 'edge_index': jax.random.randint(ks[1], (2, E), 0, N, dtype=jnp.int64)}
        for i in range(3):
            kW = jax.random.fold_in(ks[2], i)
            inp[f'W{i}'] = jax.random.normal(kW, (D, D), dtype=jnp.float32) / np.sqrt(D)
            inp[f'b{i}'] = jnp.zeros((D,), dtype=jnp.float32)
            inp[f'gamma{i}'] = jnp.ones((D,), dtype=jnp.float32)
            inp[f'beta{i}'] = jnp.zeros((D,), dtype=jnp.float32)
        return inp
    _L1_gnn_all = _L1_gnn_setup()
    _L1_gnn_in = {k: v for k, v in _L1_gnn_all.items() if k in ('W0', 'b0', 'gamma0', 'beta0', 'W1', 'b1', 'gamma1', 'beta1', 'W2', 'b2', 'gamma2', 'beta2')}
    del _L1_gnn_all

    def _L2_gnn_setup():
        import jax, jax.numpy as jnp
        import numpy as np
        N_NODES = 6250
        N_EDGES = 100000
        N_CHANNELS = 64
        HIDDEN_DIM = 32
        POLY_DEGREE = 5
        DEG_CLAMP = 1000000.0
        key = jax.random.key(seed)
        k1, k2, k3, k4, k5, k6 = jax.random.split(key, 6)
        x = jax.random.normal(k1, (N_NODES, N_CHANNELS), dtype=jnp.float32)
        edge_index = jax.random.randint(k2, (2, N_EDGES), 0, N_NODES, dtype=jnp.int32)
        fan1 = N_CHANNELS + 4
        W1 = jax.random.uniform(k3, (HIDDEN_DIM, fan1), jnp.float32, -1.0, 1.0) / np.sqrt(fan1)
        b1 = jax.random.uniform(k4, (HIDDEN_DIM,), jnp.float32, -1.0, 1.0) / np.sqrt(fan1)
        W2 = jax.random.uniform(k5, (POLY_DEGREE + 1, HIDDEN_DIM), jnp.float32, -1.0, 1.0) / np.sqrt(HIDDEN_DIM)
        b2 = jax.random.uniform(k6, (POLY_DEGREE + 1,), jnp.float32, -1.0, 1.0) / np.sqrt(HIDDEN_DIM)
        return {'x': x, 'edge_index': edge_index, 'W1': W1, 'b1': b1, 'W2': W2, 'b2': b2}
    _L2_gnn_all = _L2_gnn_setup()
    _L2_gnn_in = {k: v for k, v in _L2_gnn_all.items() if k in ('W1', 'b1', 'W2', 'b2')}
    del _L2_gnn_all

    def _L3_gnn_setup():
        import jax, jax.numpy as jnp
        import numpy as np
        N_NODES = 6250
        N_EDGES = 100000
        IN_CH = 64
        HID_CH = 64

        def _gcn_layer(x, src, dst, W, b, num_nodes):
            h = x @ W
            msgs = h[src]
            agg = jax.ops.segment_sum(msgs, dst, num_segments=num_nodes)
            return agg + b
        key = jax.random.key(seed)
        k1, k2, k3, k4, k5, k6 = jax.random.split(key, 6)
        v0 = jax.random.normal(k1, (N_NODES, IN_CH), dtype=jnp.float32)
        edge_index = jax.random.randint(k2, (2, N_EDGES), 0, N_NODES, dtype=jnp.int64)
        W1 = jax.random.normal(k3, (IN_CH, HID_CH), dtype=jnp.float32) / np.sqrt(IN_CH)
        b1 = jnp.zeros((HID_CH,), dtype=jnp.float32)
        W2 = jax.random.normal(k4, (HID_CH, HID_CH), dtype=jnp.float32) / np.sqrt(HID_CH)
        b2 = jnp.zeros((HID_CH,), dtype=jnp.float32)
        return {'v0': v0, 'edge_index': edge_index, 'W1': W1, 'b1': b1, 'W2': W2, 'b2': b2}
    _L3_gnn_all = _L3_gnn_setup()
    _L3_gnn_in = {k: v for k, v in _L3_gnn_all.items() if k in ('W1', 'b1', 'W2', 'b2')}
    del _L3_gnn_all
    return {'x': x, 'src': src, 'dst': dst, 'edge_attr_64': edge_attr_64, 'L0_gnn_W': _L0_gnn_in['W'], 'L0_gnn_b': _L0_gnn_in['b'], 'L1_gnn_W0': _L1_gnn_in['W0'], 'L1_gnn_b0': _L1_gnn_in['b0'], 'L1_gnn_gamma0': _L1_gnn_in['gamma0'], 'L1_gnn_beta0': _L1_gnn_in['beta0'], 'L1_gnn_W1': _L1_gnn_in['W1'], 'L1_gnn_b1': _L1_gnn_in['b1'], 'L1_gnn_gamma1': _L1_gnn_in['gamma1'], 'L1_gnn_beta1': _L1_gnn_in['beta1'], 'L1_gnn_W2': _L1_gnn_in['W2'], 'L1_gnn_b2': _L1_gnn_in['b2'], 'L1_gnn_gamma2': _L1_gnn_in['gamma2'], 'L1_gnn_beta2': _L1_gnn_in['beta2'], 'L2_gnn_W1': _L2_gnn_in['W1'], 'L2_gnn_b1': _L2_gnn_in['b1'], 'L2_gnn_W2': _L2_gnn_in['W2'], 'L2_gnn_b2': _L2_gnn_in['b2'], 'L3_gnn_W1': _L3_gnn_in['W1'], 'L3_gnn_b1': _L3_gnn_in['b1'], 'L3_gnn_W2': _L3_gnn_in['W2'], 'L3_gnn_b2': _L3_gnn_in['b2']}

def reference(x, src, dst, edge_attr_64, L0_gnn_W, L0_gnn_b, L1_gnn_W0, L1_gnn_b0, L1_gnn_gamma0, L1_gnn_beta0, L1_gnn_W1, L1_gnn_b1, L1_gnn_gamma1, L1_gnn_beta1, L1_gnn_W2, L1_gnn_b2, L1_gnn_gamma2, L1_gnn_beta2, L2_gnn_W1, L2_gnn_b1, L2_gnn_W2, L2_gnn_b2, L3_gnn_W1, L3_gnn_b1, L3_gnn_W2, L3_gnn_b2):
    import jax
    import jax.numpy as jnp

    def _L0_gnn_ref(h, e, src, dst, W, b):
        import jax, jax.numpy as jnp
        import numpy as np
        N_NODES = 6250
        N_EDGES = 100000
        D_IN = 64
        D_OUT = 64
        n_nodes = h.shape[0]
        msg = h[src] * e
        summed = jax.ops.segment_sum(msg, dst, num_segments=n_nodes)
        cnt = jax.ops.segment_sum(jnp.ones((msg.shape[0],), msg.dtype), dst, num_segments=n_nodes)
        h_N = summed / jnp.maximum(cnt, 1.0)[:, None]
        h_total = jnp.concatenate([h, h_N], axis=1)
        return h_total @ W.T + b

    def _L1_gnn_ref(x, edge_index, W0, b0, gamma0, beta0, W1, b1, gamma1, beta1, W2, b2, gamma2, beta2):
        import jax, jax.numpy as jnp
        import numpy as np
        N, E, D = (3125, 50000, 64)
        EPS = 1e-05

        def _gcn_norm(edge_index, n_nodes):
            loop = jnp.arange(n_nodes, dtype=edge_index.dtype)
            src = jnp.concatenate([edge_index[0], loop])
            dst = jnp.concatenate([edge_index[1], loop])
            deg = jax.ops.segment_sum(jnp.ones_like(dst, dtype=jnp.float32), dst, num_segments=n_nodes)
            dinv = jnp.where(deg > 0, jax.lax.rsqrt(deg), 0.0)
            norm = dinv[src] * dinv[dst]
            return (src, dst, norm)

        def _layer(x, src, dst, norm, W, b, gamma, beta):
            h = x @ W
            msg = h[src] * norm[:, None]
            agg = jax.ops.segment_sum(msg, dst, num_segments=x.shape[0]) + b
            mean = jnp.mean(agg, axis=0)
            var = jnp.mean(jnp.square(agg - mean), axis=0)
            y = (agg - mean) * jax.lax.rsqrt(var + EPS) * gamma + beta
            return jax.nn.elu(y)
        src, dst, norm = _gcn_norm(edge_index, x.shape[0])
        for W, b, g, bt in ((W0, b0, gamma0, beta0), (W1, b1, gamma1, beta1), (W2, b2, gamma2, beta2)):
            x = _layer(x, src, dst, norm, W, b, g, bt)
        return x

    def _L2_gnn_ref(x, edge_index, W1, b1, W2, b2):
        import jax, jax.numpy as jnp
        import numpy as np
        N_NODES = 6250
        N_EDGES = 100000
        N_CHANNELS = 64
        HIDDEN_DIM = 32
        POLY_DEGREE = 5
        DEG_CLAMP = 1000000.0
        N, C = x.shape
        E = edge_index.shape[1]
        row, col = (edge_index[0], edge_index[1])
        deg = jax.ops.segment_sum(jnp.ones((E,), x.dtype), col, num_segments=N)
        deg_inv_sqrt = jnp.minimum(deg ** (-0.5), DEG_CLAMP)
        deg_inv_sqrt = jnp.where(jnp.isinf(deg_inv_sqrt), 0.0, deg_inv_sqrt)
        norm = deg_inv_sqrt[row] * deg_inv_sqrt[col]
        x_mean = x.mean(axis=0)
        stats = jnp.stack([x.mean(), x.std(ddof=1), jnp.asarray(N, x.dtype), jnp.asarray(E, x.dtype)])
        coeff_in = jnp.concatenate([x_mean, stats])
        h = jax.nn.relu(W1 @ coeff_in + b1)
        coeffs = jax.nn.softmax(W2 @ h + b2)
        result = coeffs[0] * x
        tx = x
        for k in range(1, POLY_DEGREE + 1):
            tx = jax.ops.segment_sum(norm[:, None] * tx[col], row, num_segments=N)
            result = result + coeffs[k] * tx
        return result

    def _L3_gnn_ref(v0, edge_index, W1, b1, W2, b2):
        import jax, jax.numpy as jnp
        import numpy as np
        N_NODES = 6250
        N_EDGES = 100000
        IN_CH = 64
        HID_CH = 64

        def _gcn_layer(x, src, dst, W, b, num_nodes):
            h = x @ W
            msgs = h[src]
            agg = jax.ops.segment_sum(msgs, dst, num_segments=num_nodes)
            return agg + b
        src, dst = (edge_index[0], edge_index[1])
        n = v0.shape[0]
        x = jax.nn.relu(_gcn_layer(v0, src, dst, W1, b1, n))
        return _gcn_layer(x, src, dst, W2, b2, n)
    edge_index = jnp.stack([src, dst])
    x = _layernorm(x + _L0_gnn_ref(x, edge_attr_64, src, dst, L0_gnn_W, L0_gnn_b), axis=-1)
    x = _layernorm(x + _L1_gnn_ref(x, edge_index, L1_gnn_W0, L1_gnn_b0, L1_gnn_gamma0, L1_gnn_beta0, L1_gnn_W1, L1_gnn_b1, L1_gnn_gamma1, L1_gnn_beta1, L1_gnn_W2, L1_gnn_b2, L1_gnn_gamma2, L1_gnn_beta2), axis=-1)
    x = _layernorm(x + _L2_gnn_ref(x, edge_index, L2_gnn_W1, L2_gnn_b1, L2_gnn_W2, L2_gnn_b2), axis=-1)
    x = _layernorm(x + _L3_gnn_ref(x, edge_index, L3_gnn_W1, L3_gnn_b1, L3_gnn_W2, L3_gnn_b2), axis=-1)
    return x

_drawn_inputs = setup_inputs


def setup_inputs(seed=0):
    import zlib

    import numpy as np

    out = dict(_drawn_inputs(seed))
    spreads = {'L0_gnn_b': (0.0, 0.1),
     'L1_gnn_b0': (0.0, 0.8),
     'L1_gnn_gamma0': (1.0, 0.2),
     'L1_gnn_beta0': (0.0, 0.638),
     'L1_gnn_b1': (0.0, 0.8),
     'L1_gnn_gamma1': (1.0, 0.2),
     'L1_gnn_beta1': (0.0, 0.398),
     'L1_gnn_b2': (0.0, 0.8),
     'L1_gnn_gamma2': (1.0, 0.2),
     'L1_gnn_beta2': (0.0, 0.1),
     'L3_gnn_b1': (0.0, 0.624),
     'L3_gnn_b2': (0.0, 0.8)}
    factors = {}
    for name, (base, spread) in spreads.items():
        noise = np.random.default_rng([zlib.crc32(name.encode()), seed]).standard_normal(out[name].shape)
        drawn = base * np.exp(spread * noise) if base else spread * noise
        out[name] = jnp.asarray(drawn.astype(out[name].dtype))
    for name, factor in factors.items():
        out[name] = (out[name] * factor).astype(out[name].dtype)
    return out
```

```python
from contextlib import ExitStack

import concourse.bass as bass
from concourse import mybir

F32 = mybir.dt.float32
F16 = mybir.dt.float16
BF16 = mybir.dt.bfloat16
I32 = mybir.dt.int32
ALU = mybir.AluOpType
ACT = mybir.ActivationFunctionType
AX = mybir.AxisListType

P = 128
N = 6250
NE = 206250
D = 64
NT = 49
NP_ = NT * P
NB = 403
NC = NB * 4
WD = 8
WC = WD * NT
NW = NP_ // WD
WPT = P // WD
BPT = 8
RX = 4
QS = 4
NPASS = 10
NSLOT = 7
HALF = [(0, 25), (25, 49)]
EPS = 1e-5


def hold(eng, *pairs):
    vals = [(s, eng.snap(v)) for s, v in pairs]
    for s, v in vals:
        eng.wait_ge(s, v)


class Chain:

    def __init__(self, eng, sem):
        self.eng, self.sem, self.n = eng, sem, 0

    def op(self, ins):
        self.n += 1
        ins.then_inc(self.sem, 1)
        return (self.sem, self.n)

    def here(self):
        return (self.sem, self.n)

    def wait(self, *marks):
        for s, v in marks:
            self.eng.wait_ge(s, v)


def build(nc, I, out):
    with ExitStack() as G:
        def sb(ctx, name, shape, dt):
            return ctx.enter_context(nc.sbuf_tensor(name, shape, dt))

        def ps(ctx, name, shape, dt):
            return ctx.enter_context(nc.psum_tensor(name, shape, dt))

        def sem(name):
            return G.enter_context(nc.semaphore(name))

        a_fwd = nc.dram_tensor("a_fwd", (NT, P, NT * P), BF16).ap()
        a_bwd = nc.dram_tensor("a_bwd", (NT, P, NT, P), BF16).ap()
        d_win = nc.dram_tensor("d_win", (7, P, 2), I32).ap()
        d_blk = nc.dram_tensor("d_blk", (QS, P, 2), I32).ap()

        X = sb(G, "X", [P, NT, D], F32)
        S = sb(G, "S", [P, NT, D + 1], F32)
        ident = sb(G, "ident", [P, P], F32)
        identb = sb(G, "identb", [P, P], BF16)
        M = sb(G, "M", [P, P], F32)

        AB = ExitStack()
        Kn = sb(AB, "Kn", [P, NC + 8], F32)
        Ln = sb(AB, "Ln", [P, NC + 8], F32)
        dstp = sb(AB, "dstp", [P, NB, 4], F32)
        srci = sb(AB, "srci", [P, NB, 4], I32)
        tabw = sb(AB, "tabw", [1, 7 * P * 2], I32)
        tabb = sb(AB, "tabb", [1, QS * P * 2], I32)
        iotaw = sb(AB, "iotaw", [P, WC], F16)
        iotap = sb(AB, "iotap", [P, P], F32)
        iotah = sb(AB, "iotah", [P, P], F16)
        wtab = sb(AB, "wtab", [P, NW], F32)
        ttab = sb(AB, "ttab", [P, NT], F32)

        prep(nc, I, sem, sb, ps, locals())
        edges(nc, I, sem, sb, ps, locals())
        AB.close()
        layers(nc, I, out, sem, sb, ps, locals())


def prep(nc, I, sem, sb, ps, V):
    Kn, Ln, dstp, srci = V["Kn"], V["Ln"], V["dstp"], V["srci"]
    ident, identb, M, X, S = V["ident"], V["identb"], V["M"], V["X"], V["S"]
    iotaw, iotap, iotah, wtab, ttab = V["iotaw"], V["iotap"], V["iotah"], V["wtab"], V["ttab"]
    tabw, tabb, d_win, d_blk = V["tabw"], V["tabb"], V["d_win"], V["d_blk"]
    REG = [(P, slice(0, 3)), (NB - 3 * P, slice(3, 4))]
    with ExitStack() as C:
        si = sb(C, "si", [P, QS, 512], I32)
        di = sb(C, "di", [P, QS, 512], I32)
        hi = sb(C, "hi", [P, QS, 512], I32)
        lo = sb(C, "lo", [P, QS, 512], I32)
        sf = sb(C, "sf", [P, QS, 512], F32)
        df = sb(C, "df", [P, QS, 512], F32)
        kf = sb(C, "kf", [P, QS, 512], F32)
        lf = sb(C, "lf", [P, QS, 512], F32)
        cmx = sb(C, "cmx", [P, QS, 4], F32)
        cmn = sb(C, "cmn", [P, QS, 4], F32)
        bmx = sb(C, "bmx", [P, QS], F32)
        bmn = sb(C, "bmn", [P, QS], F32)
        bi = sb(C, "bi", [P, QS, 2], I32)
        bj = sb(C, "bj", [P, QS, 2], I32)
        cxB = sb(C, "cxB", [P, NC], F32)
        cnB = sb(C, "cnB", [P, NC], F32)
        mk = sb(C, "mk", [P, NC], F32)
        m2 = sb(C, "m2", [P, NC], F32)
        up = sb(C, "up", [P, NC], F32)
        dn = sb(C, "dn", [P, NC], F32)
        it = sb(C, "it", [P, NC], I32)
        itw = sb(C, "itw", [P, NW], I32)
        itx = sb(C, "itx", [P, WC], I32)
        itp = sb(C, "itp", [P, P], I32)
        itt = sb(C, "itt", [P, NT], I32)
        itg = sb(C, "itg", [P, 7], I32)
        lo7 = sb(C, "lo7", [P, 7], F32)
        hi7 = sb(C, "hi7", [P, 7], F32)
        r1 = sb(C, "r1", [P, 7], F32)
        r0 = sb(C, "r0", [P, 7], F32)
        wi = sb(C, "wi", [P, 7, 2], I32)
        wj = sb(C, "wj", [P, 7, 2], I32)
        wf = sb(C, "wf", [P, 7, 2], F32)
        bank = [ps(C, f"pa{i}", [P, 512], F32) for i in range(4)]
        s_ld, s_gp, s_pe, s_v, s_a, s_tb, s_x = (sem(f"a_{n}") for n in ("ld", "gp", "pe", "v", "a", "tb", "x"))

        b = C.enter_context(nc.Block())

        V_EDGE, V_BLK, V_WIN = [], [], []

        @b.vector
        def _(e):
            c = Chain(e, s_v)
            c.op(e.memset(S[:, :, :], 0.0))
            c.op(e.memset(Kn[:, NC:NC + 8], -1.0))
            c.op(e.memset(Ln[:, NC:NC + 8], -1.0))
            e.wait_ge(s_ld, 64)
            for k, q in REG:
                c.op(e.tensor_scalar(hi[0:k, q, :], si[0:k, q, :], 7, None, ALU.logical_shift_right))
                c.op(e.tensor_scalar(lo[0:k, q, :], si[0:k, q, :], 127, None, ALU.bitwise_and))
                c.op(e.tensor_copy(df[0:k, q, :], di[0:k, q, :]))
                c.op(e.tensor_copy(sf[0:k, q, :], si[0:k, q, :]))
            c.wait(c.here())
            for k, q in REG:
                c.op(e.scalar_tensor_tensor(out=kf[0:k, q, :], in0=df[0:k, q, :], scalar=float(NT),
                                            in1=hi[0:k, q, :], op0=ALU.mult, op1=ALU.add))
                c.op(e.tensor_copy(lf[0:k, q, :], lo[0:k, q, :]))
                d4 = df[0:k, q, :].rearrange("p q (m n) -> p q m n", m=4)
                c.op(e.tensor_reduce(cmx[0:k, q, :], d4, AX.X, ALU.max))
                c.op(e.tensor_reduce(cmn[0:k, q, :], d4, AX.X, ALU.min))
            V_EDGE.append(c.n)
            c.wait(c.here())
            for k, q in REG:
                c.op(e.tensor_reduce(bmx[0:k, q], cmx[0:k, q, :], AX.X, ALU.max))
                c.op(e.tensor_reduce(bmn[0:k, q], cmn[0:k, q, :], AX.X, ALU.min))
            c.wait(c.here())
            for k, q in REG:
                c.op(e.tensor_copy(bj[0:k, q, 0], bmn[0:k, q]))
                c.op(e.tensor_scalar(bj[0:k, q, 1], bmx[0:k, q], float(NP_ - 1), None, ALU.min))
            c.wait(c.here())
            for k, q in REG:
                c.op(e.tensor_scalar(bi[0:k, q, :], bj[0:k, q, :], 7, None, ALU.logical_shift_right))
            c.wait(c.here())
            for k, q in REG:
                c.op(e.tensor_scalar(bi[0:k, q, 1], bi[0:k, q, 1], 1.0, None, ALU.add))
            V_BLK.append(c.n)
            e.wait_ge(s_gp, 12)
            c.op(e.tensor_copy(wtab[:, :], itw[:, :]))
            c.op(e.tensor_copy(iotaw[:, :], itx[:, :]))
            c.op(e.tensor_copy(iotap[:, :], itp[:, :]))
            c.op(e.tensor_copy(iotah[:, :], itp[:, :]))
            c.op(e.tensor_copy(ttab[:, :], itt[:, :]))
            c.op(e.tensor_copy(lo7[:, :], itg[:, :]))
            c.op(e.tensor_scalar(up[:, :], it[:, :], 1.0, None, ALU.add))
            c.op(e.tensor_scalar(dn[:, :], it[:, :], -1.0, float(NC), ALU.mult, ALU.add))
            c.wait(c.here())
            c.op(e.tensor_scalar(hi7[:, :], lo7[:, :], float(WD - 1), None, ALU.add))
            c.wait(c.here())
            e.wait_ge(s_a, 24)
            for g in range(7):
                c.op(e.tensor_scalar(m2[:, :], cnB[:, :], hi7[:, g:g + 1], None, ALU.is_le))
                c.wait(c.here())
                c.op(e.scalar_tensor_tensor(out=mk[:, :], in0=cxB[:, :], scalar=lo7[:, g:g + 1], in1=m2[:, :],
                                            op0=ALU.is_ge, op1=ALU.mult))
                c.wait(c.here())
                c.op(e.tensor_tensor(m2[:, :], mk[:, :], up[:, :], ALU.mult))
                c.wait(c.here())
                c.op(e.tensor_reduce(r1[:, g:g + 1], m2[:, :], AX.X, ALU.max))
                c.op(e.tensor_tensor(mk[:, :], mk[:, :], dn[:, :], ALU.mult))
                c.wait(c.here())
                c.op(e.tensor_reduce(r0[:, g:g + 1], mk[:, :], AX.X, ALU.max))
            c.wait(c.here())
            c.op(e.tensor_scalar(wf[:, :, 0], r0[:, :], -1.0, float(NC), ALU.mult, ALU.add))
            c.wait(c.here())
            c.op(e.tensor_tensor(wf[:, :, 1], r1[:, :], wf[:, :, 0], ALU.subtract))
            c.wait(c.here())
            c.op(e.tensor_scalar(wf[:, :, 1], wf[:, :, 1], 1.0, 3.0, ALU.max, ALU.add))
            c.wait(c.here())
            c.op(e.tensor_copy(wj[:, :, :], wf[:, :, :]))
            c.wait(c.here())
            c.op(e.tensor_copy(wi[:, :, 0], wj[:, :, 0]))
            c.op(e.tensor_scalar(wj[:, :, 1], wj[:, :, 1], -4, None, ALU.bitwise_and))
            c.wait(c.here())
            c.op(e.tensor_tensor(wi[:, :, 1], wf[:, :, 0], wj[:, :, 1], ALU.add))
            V_WIN.append(c.n)
            c.wait(c.here())

        @b.sync
        def _(e):
            for dst, src in ((si, I["src"]), (di, I["dst"])):
                e.dma_start(dst[:, 0:3, :], src[0:3 * P, :].rearrange("(q p) n -> p q n", p=P)).then_inc(s_ld, 16)
                e.dma_start(dst[0:NB - 3 * P, 3, :], src[3 * P:NB, :]).then_inc(s_ld, 16)
            e.dma_start(X[:, :, :], I["x"].rearrange("(t p) f -> p t f", p=P)).then_inc(s_x, 16)
            e.wait_ge(s_v, V_BLK[0])
            for q in range(QS):
                n = min(P, NB - q * P)
                e.dma_start(d_blk[q, 0:n, :], bi[0:n, q, :]).then_inc(s_tb, 16)
            e.wait_ge(s_v, V_WIN[0])
            e.dma_start(d_win.rearrange("g p k -> p g k"), wi[:, :, :]).then_inc(s_tb, 16)
            e.wait_ge(s_tb, 16 * (QS + 1))
            e.dma_start(tabw[:, :], d_win.rearrange("g p k -> (g p k)").rearrange("(a n) -> a n", a=1)).then_inc(s_tb, 16)
            e.dma_start(tabb[:, 0:2 * NB], d_blk.rearrange("q p k -> (q p k)")[0:2 * NB].rearrange("(a n) -> a n", a=1)).then_inc(s_tb, 16)
            e.wait_ge(s_tb, 16 * (QS + 3))
            e.wait_ge(s_x, 16)

        @b.gpsimd
        def _(e):
            g = Chain(e, s_gp)
            g.op(e.memset(ident[:, :], 0.0))
            g.op(e.memset(identb[:, :], 0.0))
            g.op(e.memset(M[:, :], 1.0))
            g.wait(g.here())
            g.op(e.affine_select(out=ident[:, :], in_=ident[:, :], compare_op=ALU.not_equal, fill=1.0,
                                 base=0, pattern=[[-1, P]], channel_multiplier=1))
            g.op(e.affine_select(out=identb[:, :], in_=identb[:, :], compare_op=ALU.not_equal, fill=1.0,
                                 base=0, pattern=[[-1, P]], channel_multiplier=1))
            last = N - (NT - 1) * P
            g.op(e.affine_select(out=M[:, :], in_=M[:, :], compare_op=ALU.is_ge, fill=0.0,
                                 base=last - 1, pattern=[[0, P]], channel_multiplier=-1))
            g.op(e.iota(it[:, :], pattern=[[1, NC]], base=0, channel_multiplier=0))
            g.op(e.iota(itw[:, :], pattern=[[WC, NW]], base=0, channel_multiplier=0))
            g.op(e.iota(itx[:, :], pattern=[[1, WC]], base=0, channel_multiplier=0))
            g.op(e.iota(itp[:, :], pattern=[[1, P]], base=0, channel_multiplier=0))
            g.op(e.iota(itt[:, :], pattern=[[P, NT]], base=0, channel_multiplier=0))
            g.op(e.iota(itg[:, :], pattern=[[WD * P, 7]], base=0, channel_multiplier=WD))

        tp = [(a, m) for a in range(4) for m in range(4)]
        rows = [(a, m) for a in range(2) for m in range(4)]

        @b.tensor
        def _(e):
            e.wait_ge(s_gp, 12)
            e.wait_ge(s_v, V_EDGE[0])
            n = 0
            for a, m in tp:
                if n >= 4:
                    e.wait_ge(s_a, n - 3)
                for q in range(QS):
                    k = min(P, NB - q * P)
                    src = (kf, lf, df, sf)[a]
                    v = src[0:k, q, m * P:(m + 1) * P] if a < 2 else src[0:k, q, m:512:4]
                    ins = e.transpose(bank[n % 4][:, q * P:q * P + k], v, ident[0:k, 0:k])
                ins.then_inc(s_pe, 1)
                n += 1
            for a, m in rows:
                e.wait_ge(s_a, n - 3)
                for q in range(QS):
                    k = min(P, NB - q * P)
                    c = (cmx, cmn)[a]
                    ins = e.matmul(bank[n % 4][:, q * P:q * P + k], c[0:k, q, m:m + 1].to_broadcast([k, P]),
                                   ident[0:k, 0:k], start=True, stop=True)
                ins.then_inc(s_pe, 1)
                n += 1

        @b.scalar
        def _(e):
            n = 0
            for a, m in tp:
                e.wait_ge(s_pe, n + 1)
                src = bank[n % 4][:, 0:NB]
                if a < 2:
                    d = (Kn, Ln)[a][:, 0:NC].rearrange("p (b m) -> p b m", m=4)[:, :, m]
                else:
                    d = (dstp, srci)[a - 2][:, :, m]
                e.activation(d, src, ACT.Copy).then_inc(s_a, 1)
                n += 1
            for a, m in rows:
                e.wait_ge(s_pe, n + 1)
                d = (cxB, cnB)[a][:, :].rearrange("p (b m) -> p b m", m=4)[:, :, m]
                e.activation(d, bank[n % 4][:, 0:NB], ACT.Copy).then_inc(s_a, 1)
                n += 1


def edges(nc, I, sem, sb, ps, V):
    Kn, Ln, dstp, srci = V["Kn"], V["Ln"], V["dstp"], V["srci"]
    ident, identb, S = V["ident"], V["identb"], V["S"]
    iotaw, iotap, iotah, wtab, ttab = V["iotaw"], V["iotap"], V["iotah"], V["wtab"], V["ttab"]
    tabw, tabb, a_fwd, a_bwd = V["tabw"], V["tabb"], V["a_fwd"], V["a_bwd"]
    with ExitStack() as C:
        xg = [sb(C, f"xg{r}", [P, 4, D], F32) for r in range(RX)]
        eg = [sb(C, f"eg{r}", [P, 4 * D], F32) for r in range(RX)]
        msg = [sb(C, f"msg{r}", [P, 4, D + 1], F32) for r in range(2)]
        oh = [sb(C, f"oh{r}", [P, 4, P], F32) for r in range(2)]
        wk = [sb(C, f"wk{r}", [P, 4, WC], BF16) for r in range(2)]
        wl = [sb(C, f"wl{r}", [P, 4, P], BF16) for r in range(2)]
        stage = sb(C, "stage", [P, 2, NT, P], BF16)
        stgT = sb(C, "stgT", [P, NT, P], BF16)
        pw = [ps(C, f"pw{r}", [P, 512], F32) for r in range(2)]
        pm = [ps(C, f"pm{r}", [P, 512], F32) for r in range(2)]
        pt = [ps(C, f"pt{r}", [P, 1024], BF16) for r in range(2)]
        s_x = [sem(f"b_x{r}") for r in range(RX)]
        s_e = [sem(f"b_e{r}") for r in range(RX)]
        s_use, s_one = sem("b_use"), sem("b_one")
        s_oh, s_mm, s_sv = sem("b_oh"), sem("b_mm"), sem("b_sv")
        s_wo, s_wm, s_wv = sem("b_wo"), sem("b_wm"), sem("b_wv")
        s_tt, s_te = sem("b_tt"), sem("b_te")
        s_af, s_ab, s_free = sem("b_af"), sem("b_ab"), sem("b_free")

        def tiles(e, k):
            return (e.value_load(tabb[0:1, bass.ds(2 * k, 1)], min_val=0, max_val=NT - 1),
                    e.value_load(tabb[0:1, bass.ds(2 * k + 1, 1)], min_val=1, max_val=NT))

        def chunks(e, w):
            return (e.value_load(tabw[0:1, bass.ds(2 * w, 1)], min_val=0, max_val=NC),
                    e.value_load(tabw[0:1, bass.ds(2 * w + 1, 1)], min_val=4, max_val=NC + 4))

        b = C.enter_context(nc.Block())

        @b.sync
        def _(e):
            for k in range(NB):
                if k >= RX:
                    e.wait_ge(s_use, k - RX + 1)
                e.dma_start(eg[k % RX][:, :], I["e"][k]).then_inc(s_e[k % RX], 16)
                t = k // BPT - 1
                if t >= 0 and t < NT and k % BPT == 5:
                    e.wait_ge(s_wv, WPT * t + WPT + 2)
                    e.dma_start(a_fwd[t], stage[:, t % 2, :, :].rearrange("p s n -> p (s n)")).then_inc(s_af, 16)
                    e.wait_ge(s_te, 7 * t + 9)
                    e.dma_start(a_bwd[:, :, t, :].rearrange("s p l -> p s l"), stgT[:, :, :]).then_inc(s_ab, 16)
                if t >= 0 and t < NT and k % BPT == 7:
                    e.wait_ge(s_af, 16 * (t + 1))
                    e.wait_ge(s_ab, 16 * (t + 1))
                    e.sem_inc(s_free, 1)

        @b.gpsimd
        def _(e):
            for k in range(NB):
                if k >= RX:
                    e.wait_ge(s_use, k - RX + 1)
                for m in range(4):
                    e.indirect_dma_start(xg[k % RX][:, m, :], None, I["x"],
                                         bass.IndirectOffsetOnAxis(ap=srci[:, k, m:m + 1], axis=0)) \
                        .then_inc(s_x[k % RX], 16)

        @b.vector
        def _(e):
            for r in range(2):
                e.memset(msg[r][:, :, D:D + 1], 1.0).then_inc(s_one, 1)
            kk, kp, wv = (e.alloc_register(n) for n in ("v_kk", "v_kp", "v_wv"))
            wk_k, wk_p, wk_v = (e.alloc_register(n) for n in ("v_wk", "v_wp", "v_ww"))
            for r in (kk, kp, wk_k, wk_p):
                e.reg_mov(r, 0)

            def block(t, u):
                k = t * BPT + u
                r, h = u % RX, u % 2
                i = t * (BPT // RX) + u // RX + 1
                e.reg_add(wv, kp, 2)
                e.reg_mov(kp, kk)
                t0, t1 = tiles(e, k)
                hold(e, (s_x[r], 64 * i), (s_e[r], 16 * i), (s_mm, wv))
                e.tensor_tensor(msg[h][:, :, 0:D], xg[r][:, :, :], eg[r][:, :].rearrange("p (m f) -> p m f", m=4),
                                ALU.mult).then_inc(s_use, 1)
                with e.Fori(t0, t1) as j:
                    hold(e, (s_mm, wv))
                    for m in range(4):
                        ins = e.tensor_scalar(oh[h][:, m, :], iotap[:, :], ttab[:, bass.ds(j, 1)],
                                              dstp[:, bass.ds(k, 1), m], ALU.add, ALU.is_equal)
                    ins.then_inc(s_oh, 1)
                    e.reg_add(kk, kk, 1)
                    e.reg_add(wv, kk, 2)

            def window(t, u):
                w = t * WPT + u
                h = u % 2
                e.reg_add(wk_v, wk_p, 2)
                e.reg_mov(wk_p, wk_k)
                c0, c1 = chunks(e, w)
                with e.Fori(c0, c1, 4) as j:
                    hold(e, (s_wm, wk_v))
                    for m in range(4):
                        c = j + m
                        e.tensor_scalar(wl[h][:, m, :], iotah[:, :], Ln[:, bass.ds(c, 1)], None, ALU.is_equal)
                        ins = e.tensor_scalar(wk[h][:, m, :], iotaw[:, :], wtab[:, bass.ds(w, 1)],
                                              Kn[:, bass.ds(c, 1)], ALU.add, ALU.is_equal)
                    ins.then_inc(s_wo, 1)
                    e.reg_add(wk_k, wk_k, 1)
                    e.reg_add(wk_v, wk_k, 2)

            with e.Fori(0, NT) as t:
                for u in range(BPT):
                    block(t, u)
                    window(t, 2 * u)
                    window(t, 2 * u + 1)
            for u in range(NB - NT * BPT):
                block(NT + u // BPT, u % BPT)

        @b.tensor
        def _(e):
            e.wait_ge(s_one, 2)
            e.sem_inc(s_mm, 2)
            e.sem_inc(s_wm, 2)
            kk, wk_k = e.alloc_register("t_kk"), e.alloc_register("t_wk")
            e.reg_mov(kk, 1)
            e.reg_mov(wk_k, 1)

            def block(t, u):
                k = t * BPT + u
                h = u % 2
                t0, t1 = tiles(e, k)
                with e.Fori(t0, t1) as j:
                    hold(e, (s_sv, kk))
                    e.matmul(pm[h][:, 0:D + 1], ident[:, :], S[:, bass.ds(j, 1), :], start=True, stop=False)
                    hold(e, (s_oh, kk))
                    for m in range(4):
                        ins = e.matmul(pm[h][:, 0:D + 1], oh[h][:, m, :], msg[h][:, m, :], start=False, stop=(m == 3))
                    ins.then_inc(s_mm, 1)
                    e.reg_add(kk, kk, 1)

            def window(t, u):
                w = t * WPT + u
                h = u % 2
                c0, c1 = chunks(e, w)

                def trip(first):
                    if first:
                        hold(e, (s_wv, w + 1), (s_wo, wk_k))
                    else:
                        hold(e, (s_wo, wk_k))
                    for m in range(4):
                        ins = e.matmul(pw[h][:, 0:WC], wl[h][:, m, :], wk[h][:, m, :],
                                       start=first and m == 0, stop=(m == 3), skip_group_check=True)
                    ins.then_inc(s_wm, 1)
                    e.reg_add(wk_k, wk_k, 1)

                trip(True)
                with e.If(c0 + 4 < c1):
                    with e.Fori(c0 + 4, c1, 4):
                        trip(False)

            with e.Fori(0, NT) as t:
                for u in range(BPT):
                    block(t, u)
                    window(t, 2 * u)
                    window(t, 2 * u + 1)
                hold(e, (s_wv, WPT * t + WPT + 2))
                for g in range(7):
                    hold(e, (s_te, 7 * t + g + 1))
                    for m in range(7):
                        ins = e.transpose(pt[g % 2][:, m * P:(m + 1) * P], stage[:, bass.ds(t % 2, 1), 7 * g + m, :],
                                          identb[:, :])
                    ins.then_inc(s_tt, 1)
            for u in range(NB - NT * BPT):
                block(NT + u // BPT, u % BPT)

        @b.scalar
        def _(e):
            e.sem_inc(s_sv, 1)
            e.sem_inc(s_wv, 2)
            e.sem_inc(s_te, 2)
            e.sem_inc(s_free, 2)
            kk, wk_k = e.alloc_register("a_kk"), e.alloc_register("a_wk")
            e.reg_mov(kk, 3)
            e.reg_mov(wk_k, 2)

            def block(t, u):
                k = t * BPT + u
                t0, t1 = tiles(e, k)
                with e.Fori(t0, t1) as j:
                    hold(e, (s_mm, kk))
                    e.activation(S[:, bass.ds(j, 1), :], pm[u % 2][:, 0:D + 1], ACT.Copy).then_inc(s_sv, 1)
                    e.reg_add(kk, kk, 1)

            def window(t, u):
                w = t * WPT + u
                c0, c1 = chunks(e, w)
                with e.Fori(c0, c1, 4):
                    e.reg_add(wk_k, wk_k, 1)
                hold(e, (s_wm, wk_k))
                e.activation(stage[:, bass.ds(t % 2, 1), :, u * WD:(u + 1) * WD],
                             pw[u % 2][:, 0:WC].rearrange("p (d h) -> p h d", h=NT), ACT.Copy).then_inc(s_wv, 1)

            with e.Fori(0, NT) as t:
                hold(e, (s_free, t + 1))
                for u in range(BPT):
                    block(t, u)
                    window(t, 2 * u)
                    window(t, 2 * u + 1)
                hold(e, (s_free, t + 2))
                for g in range(7):
                    hold(e, (s_tt, 7 * t + g + 1))
                    e.activation(stgT[:, 7 * g:7 * g + 7, :], pt[g % 2][:, 0:7 * P].rearrange("p (a n) -> p a n", a=7),
                                 ACT.Copy).then_inc(s_te, 1)
            for u in range(NB - NT * BPT):
                block(NT + u // BPT, u % BPT)


class Lines:

    def __init__(self, sems):
        self.sems, self.n = sems, {k: 0 for k in sems}
        self.q = {k: [] for k in "vatgs"}

    def put(self, eng, make, *after):
        self.n[eng] += 1
        self.q[eng].append((make, after, True))
        return (self.sems[eng], self.n[eng])

    def raw(self, eng, make, *after):
        self.q[eng].append((make, after, False))

    def run(self, eng, e):
        for make, after, counted in self.q[eng]:
            for s, v in after:
                e.wait_ge(s, v)
            ins = make(e)
            if counted:
                ins.then_inc(self.sems[eng], 1)


def layers(nc, I, out, sem, sb, ps, V):
    X, S, ident, M = V["X"], V["S"], V["ident"], V["M"]
    a_fwd, a_bwd = V["a_fwd"], V["a_bwd"].rearrange("s p a l -> s p (a l)")
    LAST = N - (NT - 1) * P
    with ExitStack() as C:
        Y = sb(C, "Y", [P, NT, D], F32)
        T = sb(C, "T", [P, NT, D], F32)
        U = sb(C, "U", [P, NT, D], F32)
        A = sb(C, "A", [P, NT, D], F32)
        R = sb(C, "R", [P, NT, D], F32)
        Z = sb(C, "Z", [P, NT, 3, D], BF16)
        slot = [sb(C, f"slot{r}", [P, 25 * P], BF16) for r in range(NSLOT)]
        tin = [sb(C, f"tin{r}", [D, 4, P], F32) for r in range(2)]
        cnt = sb(C, "cnt", [P, NT], F32)
        dv1 = sb(C, "dv1", [P, NT], F32)
        dv2 = sb(C, "dv2", [P, NT], F32)
        st = sb(C, "st", [P, 4, NT], F32)
        ones = sb(C, "ones", [P, P], F32)
        w0 = sb(C, "w0", [D, P], F32)
        w0t = sb(C, "w0t", [D, 2, D], F32)
        wmat = {n: sb(C, "m_" + n, [D, D], F32) for n in ("L1_gnn_W0", "L1_gnn_W1", "L1_gnn_W2", "L3_gnn_W1", "L3_gnn_W2")}
        rown = ["L0_gnn_b", "L3_gnn_b1", "L3_gnn_b2"] + [f"L1_gnn_{k}{i}" for k in ("b", "gamma", "beta") for i in range(3)]
        row = {n: sb(C, "r_" + n, [P, D], F32) for n in rown}
        bst = sb(C, "bst", [P, 4, D], F32)
        sc = sb(C, "sc", [P, 16], F32)
        p1 = sb(C, "p1", [32, D + 4], F32)
        p1t = sb(C, "p1t", [D, 32], F32)
        p2 = sb(C, "p2", [6, 32], F32)
        p2t = sb(C, "p2t", [32, 6], F32)
        pb1 = sb(C, "pb1", [32, 1], F32)
        pb2 = sb(C, "pb2", [P, 6], F32)
        hh = sb(C, "hh", [32, 8], F32)
        hb = sb(C, "hb", [32, P], F32)
        xm = sb(C, "xm", [D, 1], F32)
        co = sb(C, "co", [P, 3, 6], F32)
        bank = [ps(C, f"pc{i}", [P, 512], F32) for i in range(8)]
        s_w, s_out = sem("c_w"), sem("c_out")
        s_a = [sem(f"c_a{r}") for r in range(NSLOT)]
        s_pm, s_pr, s_fr = sem("c_pm"), sem("c_pr"), sem("c_fr")
        L = Lines({k: sem("c_q" + k) for k in "vatg"})
        v = lambda f, *a: L.put("v", f, *a)
        a = lambda f, *w: L.put("a", f, *w)
        t = lambda f, *w: L.put("t", f, *w)

        def nb(ap):
            return ap.unsqueeze(2).to_broadcast([P, NT, D])

        def fb(ap):
            return ap.unsqueeze(1).to_broadcast([P, NT, D])

        def tt(o, x, y, op, *w):
            return v(lambda e: e.tensor_tensor(o, x, y, op), *w)

        def ts(o, x, s1, s2, o1, o2, *w):
            if o2 is None:
                return v(lambda e: e.tensor_scalar(o, x, s1, None, o1), *w)
            return v(lambda e: e.tensor_scalar(o, x, s1, s2, o1, o2), *w)

        def red(o, x, op, *w):
            return v(lambda e: e.tensor_reduce(o, x, AX.X, op), *w)

        def rsqrt(o, x, tmp, *w):
            k = a(lambda e: e.activation(tmp, x, ACT.Sqrt), *w)
            return v(lambda e: e.reciprocal(o, tmp), k)

        loads = []
        loads.append((w0[:, :], I["L0_gnn_W"]))
        for n, m in wmat.items():
            loads.append((m[:, :], I[n]))
        for n, m in row.items():
            loads.append((m[:, :], I[n].partition_broadcast(P)))
        loads.append((p1[:, :], I["L2_gnn_W1"]))
        loads.append((p2[:, :], I["L2_gnn_W2"]))
        loads.append((pb1[:, :], I["L2_gnn_b1"].rearrange("(p a) -> p a", a=1)))
        loads.append((pb2[:, :], I["L2_gnn_b2"].partition_broadcast(P)))
        for d, s in loads:
            L.raw("g", lambda e, d=d, s=s: e.dma_start(d, s).then_inc(s_w, 16))
        wl = (s_w, 16 * len(loads))

        npass = [0]

        def aggregate(src, back, *after):
            p = npass[0]
            npass[0] += 1
            k1 = v(lambda e: e.tensor_copy(Z[:, :, 0, :], src), *after)
            k2 = tt(T[:, :, :], src, Z[:, :, 0, :], ALU.subtract, k1)
            k3 = v(lambda e: e.tensor_copy(Z[:, :, 1, :], T[:, :, :]), k2)
            k4 = tt(Z[:, :, 2, :], T[:, :, :], Z[:, :, 1, :], ALU.subtract, k3)
            adj = a_bwd if back else a_fwd

            def load(e):
                with e.Fori(0, 7) as i:
                    for r in range(14):
                        c0, c1 = HALF[r % 2]
                        hold(e, (s_fr, 14 * i + (14 * 7 * p + r + 1)))
                        e.dma_start(slot[r % NSLOT][:, 0:(c1 - c0) * P],
                                    adj[bass.ds(i * 7 + r // 2, 1), :, c0 * P:c1 * P].rearrange("a p n -> (a p) n")) \
                            .then_inc(s_a[r % NSLOT], 16)

            def mul(e):
                with e.Fori(0, 7) as i:
                    for q in range(7):
                        hold(e, (s_pr, 7 * i + (NT * p + q + 1)))
                        for h, (c0, c1) in enumerate(HALF):
                            r = 2 * q + h
                            hold(e, (s_a[r % NSLOT], 32 * i + (16 * (14 * p + r // NSLOT + 1))))
                            for c in range(c0, c1):
                                ins = e.matmul(bank[q][:, 0:3 * D], slot[r % NSLOT][:, (c - c0) * P:(c - c0 + 1) * P],
                                               Z[:, c, :, :].rearrange("p a f -> p (a f)"), start=(c == 0), stop=(c == NT - 1))
                            ins.then_inc(s_fr, 1)

            def add(e):
                with e.Fori(0, 7) as i:
                    for q in range(7):
                        hold(e, (s_fr, 14 * i + (98 * p + 2 * q + 2 + NSLOT)))
                        e.tensor_reduce(A[:, bass.ds(i * 7 + q, 1), :].rearrange("p a f -> p (a f)"),
                                        bank[q][:, 0:3 * D].rearrange("p (a f) -> p f a", a=3), AX.X, ALU.add) \
                            .then_inc(s_pr, 1)

            L.raw("s", load)
            L.raw("t", mul, k4)
            L.raw("v", add)
            return (s_pr, 7 + NT * (p + 1))

        def project(dst, parts, *after):
            k = len(parts)
            copied, used, moved = [], [], []
            for gi, g in enumerate(range(0, NT, 4)):
                m = min(4, NT - g)
                o = bank[4 + gi % 2]
                got = []
                for src, w in parts:
                    i = len(copied)
                    pb, ti = bank[i % 2], tin[i % 2]
                    for c in range(m):
                        f = lambda e, pb=pb, src=src, c=c, g=g: e.transpose(pb[0:D, c * P:(c + 1) * P], src[:, g + c, :], ident[:, :])
                        tr = t(f, *after, *(copied[i - 2:i - 1] if i >= 2 else ()))
                    cp = a(lambda e, pb=pb, ti=ti, m=m: e.activation(ti[:, 0:m, :], pb[0:D, 0:m * P].rearrange("p (a n) -> p a n", n=P), ACT.Copy),
                           tr, *(used[(i - 2) // k:(i - 2) // k + 1] if i >= 2 else ()))
                    copied.append(cp)
                    got.append((ti, w))
                for c in range(m):
                    for j, (ti, w) in enumerate(got):
                        f = lambda e, o=o, c=c, ti=ti, w=w, j=j: e.matmul(o[:, c * D:(c + 1) * D], ti[:, c, :], w, start=(j == 0), stop=(j == k - 1))
                        mm = t(f, cp, *(moved[gi - 2:gi - 1] if gi >= 2 else ()))
                used.append(mm)
                last = v(lambda e, o=o, g=g, m=m: e.tensor_copy(dst[:, g:g + m, :], o[:, 0:m * D].rearrange("p (a f) -> p a f", f=D)), mm)
                moved.append(last)
            return last

        def layernorm(dst, y, *after):
            s, m, q, r = (st[:, i, :] for i in range(4))
            k = red(s, y, ALU.add, *after)
            k = ts(m, s, 1.0 / D, None, ALU.mult, None, k)
            k = tt(T[:, :, :], y, nb(m), ALU.subtract, k)
            k = a(lambda e: e.activation(U[:, :, :], T[:, :, :], ACT.Square), k)
            k = red(q, U[:, :, :], ALU.add, k)
            k = ts(q, q, 1.0 / D, EPS, ALU.mult, ALU.add, k)
            k = rsqrt(r, q, s, k)
            return tt(dst, T[:, :, :], nb(r), ALU.mult, k)

        def colsum(o, src, *after):
            for c in range(NT):
                lhs = ones[:, :] if c < NT - 1 else M[:, :]
                k = t(lambda e, c=c, lhs=lhs: e.matmul(o, lhs, src[:, c, :], start=(c == 0), stop=(c == NT - 1)), *(after if c == 0 else ()))
            return k

        x3, y3, t3, u3, a3, r3 = (m[:, :, :] for m in (X, Y, T, U, A, R))
        one = v(lambda e: e.memset(ones[:, :], 1.0))

        k = v(lambda e: e.tensor_copy(cnt[:, :], S[:, :, D]))
        kd = ts(dv1[:, :], cnt[:, :], 1.0, None, ALU.add, None, k)
        kd = rsqrt(dv1[:, :], dv1[:, :], st[:, 0, :], kd)
        ke = ts(dv2[:, :], cnt[:, :], 1e-12, None, ALU.max, None, kd)
        ke = rsqrt(dv2[:, :], dv2[:, :], st[:, 1, :], ke)
        k = ts(st[:, 2, :], cnt[:, :], 1.0, None, ALU.max, None, ke)
        k = v(lambda e: e.reciprocal(st[:, 3, :], st[:, 2, :]), k)
        kh = tt(r3, S[:, :, 0:D], nb(st[:, 3, :]), ALU.mult, k)
        for h in range(2):
            k = t(lambda e, h=h: e.transpose(bank[6][0:D, h * D:(h + 1) * D], w0[:, h * D:(h + 1) * D], ident[0:D, 0:D]), wl)
        k = v(lambda e: e.tensor_copy(w0t[:, :, :], bank[6][0:D, 0:2 * D].rearrange("p (a f) -> p a f", a=2)), k)
        k = project(Y, [(X, w0t[:, 0, :]), (R, w0t[:, 1, :])], k, kh)
        k = tt(y3, y3, x3, ALU.add, k)
        k = tt(y3, y3, fb(row["L0_gnn_b"][:, :]), ALU.add, k)
        kx = layernorm(x3, y3, k)

        src, k = x3, kx
        for i in range(3):
            k = tt(y3, src, nb(dv1[:, :]), ALU.mult, k)
            k2 = aggregate(y3, False, k)
            k = tt(a3, a3, y3, ALU.add, k2)
            k = tt(a3, a3, nb(dv1[:, :]), ALU.mult, k)
            k = project(R, [(A, wmat[f"L1_gnn_W{i}"][:, :])], k, wl)
            k = tt(r3, r3, fb(row[f"L1_gnn_b{i}"][:, :]), ALU.add, k)
            k = colsum(bank[6][:, 0:D], R, k, one)
            k = ts(bst[:, 0, :], bank[6][:, 0:D], 1.0 / N, None, ALU.mult, None, k)
            kc = tt(t3, r3, fb(bst[:, 0, :]), ALU.subtract, k)
            k = a(lambda e: e.activation(u3, t3, ACT.Square), kc)
            k = colsum(bank[6][:, D:2 * D], U, k)
            k = ts(bst[:, 1, :], bank[6][:, D:2 * D], 1.0 / N, EPS, ALU.mult, ALU.add, k)
            k = rsqrt(bst[:, 2, :], bst[:, 1, :], bst[:, 0, :], k)
            k = tt(bst[:, 3, :], bst[:, 2, :], row[f"L1_gnn_gamma{i}"][:, :], ALU.mult, k)
            k = tt(t3, t3, fb(bst[:, 3, :]), ALU.mult, k)
            k = tt(t3, t3, fb(row[f"L1_gnn_beta{i}"][:, :]), ALU.add, k)
            k = ts(u3, t3, 0.0, None, ALU.min, None, k)
            k = a(lambda e: e.activation(u3, u3, ACT.Exp), k)
            k = ts(t3, t3, 0.0, -1.0, ALU.max, ALU.add, k)
            k = tt(r3, t3, u3, ALU.add, k)
            src = r3
        k = tt(y3, x3, r3, ALU.add, k)
        kx = layernorm(x3, y3, k)

        k = colsum(bank[6][:, 0:D], X, kx)
        for c in range(NT):
            k = t(lambda e, c=c: e.matmul(bank[7][0:D, 0:1], X[:, c, :], (ones if c < NT - 1 else M)[:, 0:1], start=(c == 0), stop=(c == NT - 1)))
        km = ts(xm[:, :], bank[7][0:D, 0:1], 1.0 / N, None, ALU.mult, None, k)
        k = red(sc[:, 4:5], bank[6][:, 0:D], ALU.add, k)
        k = ts(sc[:, 0:1], sc[:, 4:5], 1.0 / (N * D), None, ALU.mult, None, k)
        k = ts(t3, x3, sc[:, 0:1], None, ALU.subtract, None, k)
        k = a(lambda e: e.activation(u3, t3, ACT.Square), k)
        k = colsum(bank[6][:, D:2 * D], U, k)
        k = red(sc[:, 5:6], bank[6][:, D:2 * D], ALU.add, k)
        k = ts(sc[:, 6:7], sc[:, 5:6], 1.0 / (N * D - 1), None, ALU.mult, None, k)
        k = a(lambda e: e.activation(sc[:, 1:2], sc[:, 6:7], ACT.Sqrt), k)
        v(lambda e: e.memset(sc[:, 2:3], float(N)))
        k3 = v(lambda e: e.memset(sc[:, 3:4], float(NE)))
        kt = t(lambda e: e.transpose(bank[7][0:D, 32:64], p1[:, 0:D], ident[0:32, 0:32]), wl, km)
        kt = t(lambda e: e.transpose(bank[7][0:32, 64:70], p2[:, :], ident[0:6, 0:6]))
        kq = v(lambda e: e.tensor_copy(p1t[:, :], bank[7][0:D, 32:64]), kt)
        kq = v(lambda e: e.tensor_copy(p2t[:, :], bank[7][0:32, 64:70]))
        kt = t(lambda e: e.matmul(bank[7][0:32, 80:81], p1t[:, :], xm[:, :], start=True, stop=True), kq)
        k = tt(hh[:, 0:4], p1[:, D:D + 4], sc[0:32, 0:4], ALU.mult, k, k3, wl)
        k = red(hh[:, 4:5], hh[:, 0:4], ALU.add, k)
        k = tt(hh[:, 5:6], hh[:, 4:5], pb1[:, :], ALU.add, k)
        k = tt(hh[:, 6:7], hh[:, 5:6], bank[7][0:32, 80:81], ALU.add, k, kt)
        k = ts(hh[:, 7:8], hh[:, 6:7], 0.0, None, ALU.max, None, k)
        k = ts(hb[:, :], ones[0:32, :], hh[:, 7:8], None, ALU.mult, None, k)
        k = t(lambda e: e.matmul(bank[7][:, 96:102], hb[:, :], p2t[:, :], start=True, stop=True), k)
        k = tt(co[:, 0, :], bank[7][:, 96:102], pb2[:, :], ALU.add, k)
        k = red(sc[:, 8:9], co[:, 0, :], ALU.max, k)
        k = ts(co[:, 1, :], co[:, 0, :], sc[:, 8:9], None, ALU.subtract, None, k)
        k = a(lambda e: e.activation(co[:, 1, :], co[:, 1, :], ACT.Exp), k)
        k = red(sc[:, 9:10], co[:, 1, :], ALU.add, k)
        k = v(lambda e: e.reciprocal(sc[:, 10:11], sc[:, 9:10]), k)
        k = ts(co[:, 2, :], co[:, 1, :], sc[:, 10:11], None, ALU.mult, None, k)
        kr = ts(r3, x3, co[:, 2, 0:1], None, ALU.mult, None, k)
        src, k = x3, kr
        for i in range(1, 6):
            k = tt(y3, src, nb(dv2[:, :]), ALU.mult, k)
            k = aggregate(y3, True, k)
            k = tt(a3, a3, nb(dv2[:, :]), ALU.mult, k)
            kr = v(lambda e, i=i: e.scalar_tensor_tensor(out=r3, in0=a3, scalar=co[:, 2, i:i + 1], in1=r3, op0=ALU.mult, op1=ALU.add), k)
            src, k = a3, kr
        k = tt(y3, x3, r3, ALU.add, k)
        kx = layernorm(x3, y3, k)

        k = aggregate(x3, False, kx)
        k = project(R, [(A, wmat["L3_gnn_W1"][:, :])], k)
        k = tt(r3, r3, fb(row["L3_gnn_b1"][:, :]), ALU.add, k)
        k = ts(r3, r3, 0.0, None, ALU.max, None, k)
        k = aggregate(r3, False, k)
        k = project(R, [(A, wmat["L3_gnn_W2"][:, :])], k)
        k = tt(r3, r3, fb(row["L3_gnn_b2"][:, :]), ALU.add, k)
        k = tt(y3, x3, r3, ALU.add, k)
        kx = layernorm(x3, y3, k)


        L.raw("s", lambda e: e.dma_start(out[0:(NT - 1) * P, :].rearrange("(t p) f -> p t f", p=P), X[:, 0:NT - 1, :]).then_inc(s_out, 16), kx)
        L.raw("s", lambda e: e.dma_start(out[(NT - 1) * P:N, :], X[0:LAST, NT - 1, :]).then_inc(s_out, 16))
        L.raw("s", lambda e: e.wait_ge(s_out, 32))

        b = C.enter_context(nc.Block())

        @b.sync
        def _(e):
            L.run("s", e)

        @b.gpsimd
        def _(e):
            L.run("g", e)
            e.wait_ge(*wl)

        @b.scalar
        def _(e):
            L.run("a", e)

        @b.tensor
        def _(e):
            e.sem_inc(s_fr, NSLOT)
            L.run("t", e)

        @b.vector
        def _(e):
            e.sem_inc(s_pr, 7)
            L.run("v", e)


_WEIGHTS = ["L0_gnn_W", "L0_gnn_b"] + [f"L1_gnn_{k}{i}" for i in range(3) for k in ("W", "b", "gamma", "beta")] + \
    [f"L{j}_gnn_{k}{i}" for j in (2, 3) for i in (1, 2) for k in ("W", "b")]


def kernel(**inputs):
    import numpy as _np
    import concourse.bacc as _bacc
    from concourse import mybir as _mybir
    from concourse.bass_utils import run_bass_kernel_spmd as _run

    def padded(a, n, fill):
        a = _np.asarray(a)
        return _np.concatenate([a, _np.full((n - a.shape[0],) + a.shape[1:], fill, a.dtype)])

    laid = {
        "x": padded(inputs["x"], NP_, 0),
        "src": padded(inputs["src"], NB * 512, 0).reshape(NB, 512),
        "dst": padded(inputs["dst"], NB * 512, 8191).reshape(NB, 512),
        "e": padded(inputs["edge_attr_64"], NB * 512, 0).reshape(NB, P, 4 * D),
    }
    for n in _WEIGHTS:
        laid[n] = _np.ascontiguousarray(inputs[n])
    nc = _bacc.Bacc("TRN2", target_bir_lowering=False, num_devices=1)
    arrays, args = {}, {}
    for n, v in laid.items():
        arrays[f"in_{n}"] = v
        args[n] = nc.dram_tensor(f"in_{n}", v.shape, _mybir.dt.from_np(v.dtype), kind="ExternalInput").ap()
    out = nc.dram_tensor("out_0", (N, D), F32, kind="ExternalOutput").ap()
    build(nc, args, out)
    r = _run(nc, [arrays], core_ids=[0])
    return r.results[0]["out_0"]
```

```python
from contextlib import ExitStack

import concourse.bass as bass
from concourse import mybir

F32 = mybir.dt.float32
F16 = mybir.dt.float16
BF16 = mybir.dt.bfloat16
FP8 = mybir.dt.float8e4
I32 = mybir.dt.int32
ALU = mybir.AluOpType
ACT = mybir.ActivationFunctionType
AX = mybir.AxisListType

P = 128
N = 6250
NE = 206250
D = 64
NT = 49
NP_ = NT * P
NB = 403
NC = NB * 4
WD = 8
WC = WD * NT
NW = NP_ // WD
WPT = P // WD
BPT = 8
RX = 8
NWS = 4
CH = 3
TG = 4
CAP = 16
PL = 3
QS = 4
NPASS = 10
NSLOT = 7
EPS = 1e-5


def hold(eng, *pairs):
    vals = [(s, eng.snap(v)) for s, v in pairs]
    for s, v in vals:
        eng.wait_ge(s, v)


def values(nc, e, at):
    return nc.values_load_multi_w_load_instructions(
        at, engines=[e.engine], min_val=0, max_val=NC,
        skip_runtime_bounds_check_because="the tables hold chunk and tile numbers made on the chip")[1]


class Chain:

    def __init__(self, eng, sem):
        self.eng, self.sem, self.n = eng, sem, 0

    def op(self, ins):
        self.n += 1
        ins.then_inc(self.sem, 1)
        return (self.sem, self.n)

    def here(self):
        return (self.sem, self.n)

    def wait(self, *marks):
        for s, v in marks:
            self.eng.wait_ge(s, v)


def build(nc, I, out):
    with ExitStack() as G:
        def sb(ctx, name, shape, dt):
            return ctx.enter_context(nc.sbuf_tensor(name, shape, dt))

        def ps(ctx, name, shape, dt):
            return ctx.enter_context(nc.psum_tensor(name, shape, dt))

        def sem(name):
            return G.enter_context(nc.semaphore(name))

        a_fwd = nc.dram_tensor("a_fwd", (NT, P, NT * P), FP8).ap()
        a_bwd = nc.dram_tensor("a_bwd", (NT, P, NT * P), FP8).ap()
        g_fwd = nc.dram_tensor("g_fwd", (PL, NT, P, NT * P), BF16).ap()
        g_bwd = nc.dram_tensor("g_bwd", (PL, NT, P, NT * P), BF16).ap()
        d_win = nc.dram_tensor("d_win", (7, P, 2), I32).ap()
        d_blk = nc.dram_tensor("d_blk", (QS, P, 2), I32).ap()

        X = sb(G, "X", [P, NT, D], F32)
        S = sb(G, "S", [P, NT, D + 1], F32)
        ident = sb(G, "ident", [P, P], F32)
        identb = sb(G, "identb", [P, P], BF16)
        M = sb(G, "M", [P, P], F32)
        vio = sb(G, "vio", [P, NT], F32)
        flag = sb(G, "flag", [1, 1], I32)

        AB = ExitStack()
        Kn = sb(AB, "Kn", [P, NC + 8], F32)
        Ln = sb(AB, "Ln", [P, NC + 8], F32)
        dstp = sb(AB, "dstp", [P, NB, 4], F32)
        srci = sb(AB, "srci", [P, NB, 4], I32)
        tabw = sb(AB, "tabw", [1, 7 * P * 2], I32)
        tabb = sb(AB, "tabb", [1, QS * P * 2], I32)
        iotaw = sb(AB, "iotaw", [P, WC], F16)
        iotap = sb(AB, "iotap", [P, P], F32)
        iotah = sb(AB, "iotah", [P, P], F16)
        ttab = sb(AB, "ttab", [P, NT], F32)

        prep(nc, I, sem, sb, ps, locals())
        edges(nc, I, sem, sb, ps, locals())
        planes(nc, sem, sb, ps, locals())
        AB.close()
        layers(nc, I, out, sem, sb, ps, locals())


def prep(nc, I, sem, sb, ps, V):
    Kn, Ln, dstp, srci = V["Kn"], V["Ln"], V["dstp"], V["srci"]
    ident, identb, M, X, S = V["ident"], V["identb"], V["M"], V["X"], V["S"]
    iotaw, iotap, iotah, ttab = V["iotaw"], V["iotap"], V["iotah"], V["ttab"]
    tabw, tabb, d_win, d_blk = V["tabw"], V["tabb"], V["d_win"], V["d_blk"]
    REG = [(P, slice(0, 3)), (NB - 3 * P, slice(3, 4))]
    with ExitStack() as C:
        si = sb(C, "si", [P, QS, 512], I32)
        di = sb(C, "di", [P, QS, 512], I32)
        hi = sb(C, "hi", [P, QS, 512], I32)
        lo = sb(C, "lo", [P, QS, 512], I32)
        sf = sb(C, "sf", [P, QS, 512], F32)
        df = sb(C, "df", [P, QS, 512], F32)
        kf = sb(C, "kf", [P, QS, 512], F32)
        lf = sb(C, "lf", [P, QS, 512], F32)
        cmx = sb(C, "cmx", [P, QS, 4], F32)
        cmn = sb(C, "cmn", [P, QS, 4], F32)
        bmx = sb(C, "bmx", [P, QS], F32)
        bmn = sb(C, "bmn", [P, QS], F32)
        bi = sb(C, "bi", [P, QS, 2], I32)
        bj = sb(C, "bj", [P, QS, 2], I32)
        cxB = sb(C, "cxB", [P, NC], F32)
        cnB = sb(C, "cnB", [P, NC], F32)
        mk = sb(C, "mk", [P, NC], F32)
        m2 = sb(C, "m2", [P, NC], F32)
        itx = sb(C, "itx", [P, WC], I32)
        itp = sb(C, "itp", [P, P], I32)
        itt = sb(C, "itt", [P, NT], I32)
        itg = sb(C, "itg", [P, 7], I32)
        lo7 = sb(C, "lo7", [P, 7], F32)
        hi7 = sb(C, "hi7", [P, 7], F32)
        r1 = sb(C, "r1", [P, 7], F32)
        r0 = sb(C, "r0", [P, 7], F32)
        wi = sb(C, "wi", [P, 7, 2], I32)
        wf = sb(C, "wf", [P, 7, 2], F32)
        bank = [ps(C, f"pa{i}", [P, 512], F32) for i in range(4)]
        s_ld, s_gp, s_pe, s_v, s_a, s_tb, s_x = (sem(f"a_{n}") for n in ("ld", "gp", "pe", "v", "a", "tb", "x"))

        b = C.enter_context(nc.Block())

        V_EDGE, V_BLK, V_WIN = [], [], []

        @b.vector
        def _(e):
            c = Chain(e, s_v)
            c.op(e.memset(S[:, :, :], 0.0))
            c.op(e.memset(Kn[:, NC:NC + 8], -1.0))
            c.op(e.memset(Ln[:, NC:NC + 8], -1.0))
            e.wait_ge(s_ld, 64)
            for k, q in REG:
                c.op(e.tensor_scalar(hi[0:k, q, :], si[0:k, q, :], 7, None, ALU.logical_shift_right))
                c.op(e.tensor_scalar(lo[0:k, q, :], si[0:k, q, :], 127, None, ALU.bitwise_and))
                c.op(e.tensor_copy(df[0:k, q, :], di[0:k, q, :]))
                c.op(e.tensor_copy(sf[0:k, q, :], si[0:k, q, :]))
            c.wait(c.here())
            for k, q in REG:
                c.op(e.scalar_tensor_tensor(out=kf[0:k, q, :], in0=df[0:k, q, :], scalar=float(NT),
                                            in1=hi[0:k, q, :], op0=ALU.mult, op1=ALU.add))
                c.op(e.tensor_copy(lf[0:k, q, :], lo[0:k, q, :]))
                d4 = df[0:k, q, :].rearrange("p q (m n) -> p q m n", m=4)
                c.op(e.tensor_reduce(cmx[0:k, q, :], d4, AX.X, ALU.max))
                c.op(e.tensor_reduce(cmn[0:k, q, :], d4, AX.X, ALU.min))
            V_EDGE.append(c.n)
            c.wait(c.here())
            for k, q in REG:
                c.op(e.tensor_reduce(bmx[0:k, q], cmx[0:k, q, :], AX.X, ALU.max))
                c.op(e.tensor_reduce(bmn[0:k, q], cmn[0:k, q, :], AX.X, ALU.min))
            c.wait(c.here())
            for k, q in REG:
                c.op(e.tensor_copy(bj[0:k, q, 0], bmn[0:k, q]))
                c.op(e.tensor_scalar(bj[0:k, q, 1], bmx[0:k, q], float(NP_ - 1), None, ALU.min))
            c.wait(c.here())
            for k, q in REG:
                c.op(e.tensor_scalar(bi[0:k, q, :], bj[0:k, q, :], 7, None, ALU.logical_shift_right))
            c.wait(c.here())
            for k, q in REG:
                c.op(e.tensor_scalar(bi[0:k, q, 1], bi[0:k, q, 1], 1.0, None, ALU.add))
            V_BLK.append(c.n)
            e.wait_ge(s_gp, 10)
            c.op(e.tensor_copy(iotaw[:, :], itx[:, :]))
            c.op(e.tensor_copy(iotap[:, :], itp[:, :]))
            c.op(e.tensor_copy(iotah[:, :], itp[:, :]))
            c.op(e.tensor_copy(ttab[:, :], itt[:, :]))
            c.op(e.tensor_copy(lo7[:, :], itg[:, :]))
            c.wait(c.here())
            c.op(e.tensor_scalar(hi7[:, :], lo7[:, :], float(WD - 1), None, ALU.add))
            c.wait(c.here())
            e.wait_ge(s_a, 24)
            c.op(e.tensor_tensor_scan(mk[:, :], cxB[:, :], cxB[:, :], 0.0, ALU.max, ALU.max))
            c.op(e.tensor_tensor_scan(m2[:, ::-1], cnB[:, ::-1], cnB[:, ::-1], 1e9, ALU.min, ALU.min))
            c.wait(c.here())
            for g in range(7):
                c.wait(c.here())
                c.op(e.tensor_scalar(cxB[:, :], mk[:, :], lo7[:, g:g + 1], 0.0, ALU.is_lt, ALU.add, accum_out=r0[:, g:g + 1]))
                c.op(e.tensor_scalar(cnB[:, :], m2[:, :], hi7[:, g:g + 1], 0.0, ALU.is_le, ALU.add, accum_out=r1[:, g:g + 1]))
            c.wait(c.here())
            c.op(e.tensor_scalar(wf[:, :, 0], r0[:, :], 1.0, None, ALU.add))
            c.wait(c.here())
            c.op(e.tensor_copy(wi[:, :, 0], r0[:, :]))
            c.op(e.tensor_tensor(wi[:, :, 1], r1[:, :], wf[:, :, 0], ALU.max))
            V_WIN.append(c.n)
            c.wait(c.here())

        @b.sync
        def _(e):
            for dst, src in ((si, I["src"]), (di, I["dst"])):
                e.dma_start(dst[:, 0:3, :], src[0:3 * P, :].rearrange("(q p) n -> p q n", p=P)).then_inc(s_ld, 16)
                e.dma_start(dst[0:NB - 3 * P, 3, :], src[3 * P:NB, :]).then_inc(s_ld, 16)
            e.dma_start(X[:, :, :], I["x"].rearrange("(t p) f -> p t f", p=P)).then_inc(s_x, 16)
            e.wait_ge(s_v, V_BLK[0])
            for q in range(QS):
                n = min(P, NB - q * P)
                e.dma_start(d_blk[q, 0:n, :], bi[0:n, q, :]).then_inc(s_tb, 16)
            e.wait_ge(s_v, V_WIN[0])
            e.dma_start(d_win.rearrange("g p k -> p g k"), wi[:, :, :]).then_inc(s_tb, 16)
            e.wait_ge(s_tb, 16 * (QS + 1))
            e.dma_start(tabw[:, :], d_win.rearrange("g p k -> (g p k)").rearrange("(a n) -> a n", a=1)).then_inc(s_tb, 16)
            e.dma_start(tabb[:, 0:2 * NB], d_blk.rearrange("q p k -> (q p k)")[0:2 * NB].rearrange("(a n) -> a n", a=1)).then_inc(s_tb, 16)
            e.wait_ge(s_tb, 16 * (QS + 3))
            e.wait_ge(s_x, 16)

        @b.gpsimd
        def _(e):
            g = Chain(e, s_gp)
            g.op(e.memset(ident[:, :], 0.0))
            g.op(e.memset(identb[:, :], 0.0))
            g.op(e.memset(M[:, :], 1.0))
            g.wait(g.here())
            g.op(e.affine_select(out=ident[:, :], in_=ident[:, :], compare_op=ALU.not_equal, fill=1.0,
                                 base=0, pattern=[[-1, P]], channel_multiplier=1))
            g.op(e.affine_select(out=identb[:, :], in_=identb[:, :], compare_op=ALU.not_equal, fill=1.0,
                                 base=0, pattern=[[-1, P]], channel_multiplier=1))
            last = N - (NT - 1) * P
            g.op(e.affine_select(out=M[:, :], in_=M[:, :], compare_op=ALU.is_ge, fill=0.0,
                                 base=last - 1, pattern=[[0, P]], channel_multiplier=-1))
            g.op(e.iota(itx[:, :], pattern=[[1, WC]], base=0, channel_multiplier=0))
            g.op(e.iota(itp[:, :], pattern=[[1, P]], base=0, channel_multiplier=0))
            g.op(e.iota(itt[:, :], pattern=[[P, NT]], base=0, channel_multiplier=0))
            g.op(e.iota(itg[:, :], pattern=[[WD * P, 7]], base=0, channel_multiplier=WD))

        tp = [(a, m) for a in range(4) for m in range(4)]
        rows = [(a, m) for a in range(2) for m in range(4)]

        @b.tensor
        def _(e):
            e.wait_ge(s_gp, 10)
            e.wait_ge(s_v, V_EDGE[0])
            n = 0
            for a, m in tp:
                if n >= 4:
                    e.wait_ge(s_a, n - 3)
                for q in range(QS):
                    k = min(P, NB - q * P)
                    src = (kf, lf, df, sf)[a]
                    v = src[0:k, q, m * P:(m + 1) * P] if a < 2 else src[0:k, q, m:512:4]
                    ins = e.transpose(bank[n % 4][:, q * P:q * P + k], v, ident[0:k, 0:k])
                ins.then_inc(s_pe, 1)
                n += 1
            for a, m in rows:
                e.wait_ge(s_a, n - 3)
                for q in range(QS):
                    k = min(P, NB - q * P)
                    c = (cmx, cmn)[a]
                    ins = e.matmul(bank[n % 4][:, q * P:q * P + k], c[0:k, q, m:m + 1].to_broadcast([k, P]),
                                   ident[0:k, 0:k], start=True, stop=True)
                ins.then_inc(s_pe, 1)
                n += 1

        @b.scalar
        def _(e):
            n = 0
            for a, m in tp:
                e.wait_ge(s_pe, n + 1)
                src = bank[n % 4][:, 0:NB]
                if a < 2:
                    d = (Kn, Ln)[a][:, 0:NC].rearrange("p (b m) -> p b m", m=4)[:, :, m]
                else:
                    d = (dstp, srci)[a - 2][:, :, m]
                e.activation(d, src, ACT.Copy).then_inc(s_a, 1)
                n += 1
            for a, m in rows:
                e.wait_ge(s_pe, n + 1)
                d = (cxB, cnB)[a][:, :].rearrange("p (b m) -> p b m", m=4)[:, :, m]
                e.activation(d, bank[n % 4][:, 0:NB], ACT.Copy).then_inc(s_a, 1)
                n += 1


def edges(nc, I, sem, sb, ps, V):
    Kn, Ln, dstp, srci = V["Kn"], V["Ln"], V["dstp"], V["srci"]
    ident, identb, S, vio = V["ident"], V["identb"], V["S"], V["vio"]
    iotaw, iotap, iotah, ttab = V["iotaw"], V["iotap"], V["iotah"], V["ttab"]
    tabw, tabb, a_fwd, a_bwd = V["tabw"], V["tabb"], V["a_fwd"], V["a_bwd"]
    ENG = mybir.EngineType
    with ExitStack() as C:
        xg = [sb(C, f"xg{r}", [P, 4, D], F32) for r in range(RX)]
        eg = [sb(C, f"eg{r}", [P, 4 * D], F32) for r in range(RX)]
        msg = [sb(C, f"msg{r}", [P, 4, D + 1], F32) for r in range(2)]
        oh = [sb(C, f"oh{r}", [P, 4, P], F32) for r in range(2)]
        ohx = sb(C, "ohx", [P, 4, P], F32)
        wk = [sb(C, f"wk{r}", [P, CH, WC], BF16) for r in range(NWS)]
        wl = [sb(C, f"wl{r}", [P, CH, P], BF16) for r in range(NWS)]
        wkx = sb(C, "wkx", [P, CH, WC], BF16)
        wlx = sb(C, "wlx", [P, CH, P], BF16)
        stage = sb(C, "stage", [P, 2, NT, P], BF16)
        stg8 = sb(C, "stg8", [P, 2, NT * P], FP8)
        stgT = sb(C, "stgT", [P, NT, TG * P], FP8)
        junk = sb(C, "junk", [P, NT * P], FP8)
        ncap = sb(C, "ncap", [P, 1], F32)
        pw = [ps(C, f"pw{r}", [P, 512], F32) for r in range(3)]
        pm = [ps(C, f"pm{r}", [P, 512], F32) for r in range(2)]
        pmx = ps(C, "pmx", [P, 512], F32)
        pt = [ps(C, f"pt{r}", [P, 1024], BF16) for r in range(2)]
        s_x = [sem(f"b_x{r}") for r in range(RX)]
        s_e = [sem(f"b_e{r}") for r in range(RX)]
        s_use, s_one = sem("b_use"), sem("b_one")
        s_oh, s_mm, s_sv = sem("b_oh"), sem("b_mm"), sem("b_sv")
        s_oy, s_my, s_sy = sem("b_oy"), sem("b_my"), sem("b_sy")
        s_wo, s_wm, s_wv = sem("b_wo"), sem("b_wm"), sem("b_wv")
        s_xo, s_xm = sem("b_xo"), sem("b_xm")
        s_tt, s_te, s_c8 = sem("b_tt"), sem("b_te"), sem("b_c8")
        s_af, s_ab = sem("b_af"), sem("b_ab")

        def tiles(e, k):
            t0, t1 = values(nc, e, tabb[0:1, 2 * k:2 * k + 2])
            return t0.with_bounds(min_val=0, max_val=NT - 1), t1.with_bounds(min_val=1, max_val=NT)

        def pairs(e, k):
            v = values(nc, e, tabw[0:1, 4 * k:4 * k + 4])
            return [(v[2 * i].with_bounds(min_val=0, max_val=NC), v[2 * i + 1].with_bounds(min_val=1, max_val=NC + 1)) for i in range(2)]

        def side(t, u):
            return (t - 1, u - 1) if 1 <= t <= NT and 1 <= u <= 7 else None

        b = C.enter_context(nc.Block())

        @b.sync
        def _(e):
            for k in range(NB):
                if k >= RX:
                    e.wait_ge(s_use, k - RX + 1)
                e.dma_start(eg[k % RX][:, :], I["e"][k]).then_inc(s_e[k % RX], 16)
                t, u = divmod(k, BPT)
                if u == 4 and 1 <= t <= NT:
                    if t >= 2:
                        e.wait_ge(s_af, 16 * (t - 1))
                    e.wait_ge(s_c8, t)
                    e.dma_start(a_fwd[t - 1], stg8[:, (t - 1) % 2, :]).then_inc(s_af, 16)
                if (u == 2 and t >= 2 and (t - 1) % TG == 0) or k == NB - 1:
                    q = (t - 2) // TG if k < NB - 1 else (NT - 1) // TG
                    n = min(TG, NT - TG * q)
                    e.wait_ge(s_te, 7 * (TG * q + n))
                    e.dma_start(a_bwd[:, :, TG * q * P:(TG * q + n) * P].rearrange("s p l -> p s l"),
                                stgT[:, :, 0:n * P]).then_inc(s_ab, 16)
            e.wait_ge(s_af, 16 * NT)
            e.wait_ge(s_ab, 16 * ((NT + TG - 1) // TG))

        @b.gpsimd
        def _(e):
            for k in range(NB):
                if k >= RX:
                    e.wait_ge(s_use, k - RX + 1)
                for m in range(4):
                    e.indirect_dma_start(xg[k % RX][:, m, :], None, I["x"],
                                         bass.IndirectOffsetOnAxis(ap=srci[:, k, m:m + 1], axis=0)) \
                        .then_inc(s_x[k % RX], 16)

        @b.vector
        def _(e):
            for r in range(2):
                e.memset(msg[r][:, :, D:D + 1], 1.0).then_inc(s_one, 1)
            e.memset(ncap[:, :], -float(CAP)).then_inc(s_one, 1)
            cy, cx = e.alloc_register("v_cy"), e.alloc_register("v_cx")
            e.reg_mov(cy, 1)
            e.reg_mov(cx, 1)

            def hits(o, k, tile):
                return e.scalar_tensor_tensor(out=o[:, :, :], in0=iotap[:, :].unsqueeze(1).to_broadcast([P, 4, P]),
                                              scalar=ttab[:, bass.ds(tile, 1)],
                                              in1=dstp[:, k, :].unsqueeze(2).to_broadcast([P, 4, P]),
                                              op0=ALU.add, op1=ALU.is_equal)

            def block(k):
                r, h = k % RX, k % 2
                t0, t1 = tiles(e, k)
                e.wait_ge(s_x[r], 64 * (k // RX + 1))
                e.wait_ge(s_e[r], 16 * (k // RX + 1))
                if k >= 2:
                    e.wait_ge(s_mm, k - 1)
                e.tensor_tensor(msg[h][:, :, 0:D], xg[r][:, :, :], eg[r][:, :].rearrange("p (m f) -> p m f", m=4),
                                ALU.mult).then_inc(s_use, 1)
                with e.If(t0 + 1 < t1):
                    with e.Fori(t0 + 1, t1) as j:
                        hold(e, (s_my, cy))
                        hits(ohx, k, j).then_inc(s_oy, 1)
                        e.reg_add(cy, cy, 1)
                hits(oh[h], k, t0).then_inc(s_oh, 1)

            def marks(o, l, w, c):
                e.tensor_tensor(l[:, :, :], iotah[:, :].unsqueeze(1).to_broadcast([P, CH, P]),
                                Ln[:, bass.ds(c, CH)].unsqueeze(2).to_broadcast([P, CH, P]), ALU.is_equal)
                for m in range(CH):
                    ins = e.tensor_scalar(o[:, m, :], iotaw[:, :], float(WC * w), Kn[:, bass.ds(c + m, 1)],
                                          ALU.add, ALU.is_equal)
                return ins

            def window(w, c0, c1):
                if w >= NWS:
                    e.wait_ge(s_wm, w - NWS + 1)
                marks(wk[w % NWS], wl[w % NWS], w, c0).then_inc(s_wo, 1)
                with e.If(c0 + CH < c1):
                    with e.Fori(c0 + CH, c1, CH) as j:
                        hold(e, (s_xm, cx))
                        marks(wkx, wlx, w, j).then_inc(s_xo, 1)
                        e.reg_add(cx, cx, 1)

            for k in range(NB):
                block(k)
                if 2 * k < NW:
                    for i, c in enumerate(pairs(e, k)):
                        window(2 * k + i, *c)

        @b.tensor
        def _(e):
            e.wait_ge(s_one, 3)
            e.sem_inc(s_xm, 1)
            e.sem_inc(s_my, 1)
            cy, cx = e.alloc_register("t_cy"), e.alloc_register("t_cx")
            e.reg_mov(cy, 1)
            e.reg_mov(cx, 1)

            def gather(o, k, tile, hot):
                e.matmul(o[:, 0:D + 1], ident[:, :], S[:, bass.ds(tile, 1), :], start=True, stop=False)
                for m in range(4):
                    ins = e.matmul(o[:, 0:D + 1], hot[:, m, :], msg[k % 2][:, m, :], start=False, stop=(m == 3))
                return ins

            def block(k):
                t0, t1 = tiles(e, k)
                if k >= 1:
                    e.wait_ge(s_sv, k)
                with e.If(t0 + 1 < t1):
                    with e.Fori(t0 + 1, t1) as j:
                        hold(e, (s_sy, cy), (s_oy, cy))
                        gather(pmx, k, j, ohx).then_inc(s_my, 1)
                        e.reg_add(cy, cy, 1)
                e.wait_ge(s_oh, k + 1)
                gather(pm[k % 2], k, t0, oh[k % 2]).then_inc(s_mm, 1)

            def window(w, c0, c1):
                o = pw[w % 3][:, 0:WC]
                k, l = wk[w % NWS], wl[w % NWS]
                e.wait_ge(s_wo, w + 1)
                if w >= 3:
                    e.wait_ge(s_wv, w - 2)
                for m in range(CH - 1):
                    e.matmul(o, l[:, m, :], k[:, m, :], start=(m == 0), stop=False, skip_group_check=True)
                with e.If(c0 + CH < c1):
                    with e.Fori(c0 + CH, c1, CH):
                        hold(e, (s_xo, cx))
                        for m in range(CH):
                            ins = e.matmul(o, wlx[:, m, :], wkx[:, m, :], start=False, stop=False, skip_group_check=True)
                        ins.then_inc(s_xm, 1)
                        e.reg_add(cx, cx, 1)
                e.matmul(o, l[:, CH - 1, :], k[:, CH - 1, :], start=False, stop=True, skip_group_check=True).then_inc(s_wm, 1)

            def turn(t, g):
                n = 7 * t + g
                if g == 0:
                    e.wait_ge(s_wv, WPT * (t + 1))
                if n >= 2:
                    e.wait_ge(s_te, n - 1)
                for m in range(7):
                    ins = e.transpose(pt[n % 2][:, m * P:(m + 1) * P], stage[:, t % 2, 7 * g + m, :], identb[:, :])
                ins.then_inc(s_tt, 1)

            for k in range(NB):
                block(k)
                if 2 * k < NW:
                    for i, c in enumerate(pairs(e, k)):
                        window(2 * k + i, *c)
                if side(*divmod(k, BPT)):
                    turn(*side(*divmod(k, BPT)))

        @b.scalar
        def _(e):
            e.sem_inc(s_sy, 1)
            e.wait_ge(s_one, 3)
            cy = e.alloc_register("a_cy")
            e.reg_mov(cy, 2)

            def block(k):
                t0, t1 = tiles(e, k)
                with e.If(t0 + 1 < t1):
                    with e.Fori(t0 + 1, t1) as j:
                        hold(e, (s_my, cy))
                        e.activation(S[:, bass.ds(j, 1), :], pmx[:, 0:D + 1], ACT.Copy).then_inc(s_sy, 1)
                        e.reg_add(cy, cy, 1)
                e.wait_ge(s_mm, k + 1)
                e.activation(S[:, bass.ds(t0, 1), :], pm[k % 2][:, 0:D + 1], ACT.Copy).then_inc(s_sv, 1)

            def window(w):
                t, u = divmod(w, WPT)
                e.wait_ge(s_wm, w + 1)
                e.activation(stage[:, t % 2, :, u * WD:(u + 1) * WD],
                             pw[w % 3][:, 0:WC].rearrange("p (d h) -> p h d", h=NT), ACT.Copy).then_inc(s_wv, 1)

            def turned(t, g):
                n = 7 * t + g
                flat = stage[:, t % 2, :, :].rearrange("p s l -> p (s l)")
                if g == 0:
                    e.wait_ge(s_wv, WPT * (t + 1))
                    if t % TG == 0 and t:
                        e.wait_ge(s_ab, 16 * (t // TG))
                    if t >= 2:
                        e.wait_ge(s_af, 16 * (t - 1))
                    e.activation(stg8[:, t % 2, :], flat, ACT.Copy, saturate=False).then_inc(s_c8, 1)
                if g == 4:
                    e.activation(junk[:, :], flat, ACT.Relu, bias=ncap[:, :], accum_out=vio[:, t:t + 1], saturate=False)
                e.wait_ge(s_tt, n + 1)
                e.activation(stgT[:, 7 * g:7 * g + 7, (t % TG) * P:(t % TG + 1) * P],
                             pt[n % 2][:, 0:7 * P].rearrange("p (a n) -> p a n", a=7), ACT.Copy,
                             saturate=False).then_inc(s_te, 1)

            for k in range(NB):
                block(k)
                if 2 * k < NW:
                    window(2 * k)
                    window(2 * k + 1)
                if side(*divmod(k, BPT)):
                    turned(*side(*divmod(k, BPT)))


def planes(nc, sem, sb, ps, V):
    Kn, Ln, iotaw, iotah, tabw = V["Kn"], V["Ln"], V["iotaw"], V["iotah"], V["tabw"]
    identb, vio, flag, g_fwd, g_bwd = V["identb"], V["vio"], V["flag"], V["g_fwd"], V["g_bwd"]
    with ExitStack() as C:
        fv = sb(C, "fv", [P, 1], F32)
        onec = sb(C, "onec", [P, 1], F32)
        base = sb(C, "base", [P, 1], F32)
        gk = sb(C, "gk", [P, WC], BF16)
        gl = sb(C, "gl", [P, P], BF16)
        cw = sb(C, "cw", [P, NT, P], I32)
        dg = sb(C, "dg", [P, NT, P], I32)
        pl = sb(C, "pl", [P, NT, P], BF16)
        plT = sb(C, "plT", [P, NT, P], BF16)
        pf = ps(C, "pf", [P, 512], F32)
        pc = ps(C, "pcw", [P, 512], F32)
        pt = ps(C, "ptg", [P, 1024], BF16)
        s_c, s_f, s_m = sem("g_c"), sem("g_f"), sem("g_m")
        s_own, s_d, s_p, s_o, s_w = (sem(f"g_{n}") for n in ("own", "d", "p", "o", "w"))

        b = C.enter_context(nc.Block())

        def flagged(e):
            e.wait_ge(s_f, 1)
            return values(nc, e, flag[0:1, 0:1])[0]

        def chunks(e, t, u):
            c0, c1 = values(nc, e, tabw[0:1, bass.ds((t * WPT + u) * 2, 2)])
            return c0.with_bounds(min_val=0, max_val=NC - 1), c1.with_bounds(min_val=1, max_val=NC)

        @b.vector
        def _(e):
            c = Chain(e, s_c)
            c.op(e.memset(onec[:, :], 1.0))
            c.op(e.tensor_reduce(fv[:, :], vio[:, :], AX.X, ALU.add))
            e.wait_ge(s_m, 1)
            e.tensor_scalar(flag[0:1, 0:1], pf[0:1, 0:1], 1.0, None, ALU.min).then_inc(s_f, 1)
            go = flagged(e)
            n, m, w = (e.alloc_register("gv_" + x) for x in "nmw")
            for r in (n, m, w):
                e.reg_mov(r, 1)

            def own(ins):
                ins.then_inc(s_own, 1)
                hold(e, (s_own, m))
                e.reg_add(m, m, 1)

            def turn():
                e.sem_inc(s_d, 1)
                hold(e, (s_p, n))
                e.reg_add(n, n, 1)

            with e.If(go > 0):
                own(e.memset(base[:, :], 0.0))
                own(e.memset(gk[:, :], 0.0))
                with e.Fori(0, NT) as t:
                    with e.Fori(0, WPT) as u:
                        c0, c1 = chunks(e, t, u)
                        own(e.memset(gl[:, :], 0.0))
                        turn()
                        with e.Fori(c0, c1) as j:
                            own(e.tensor_scalar(gk[:, :], iotaw[:, :], base[:, :], Kn[:, bass.ds(j, 1)], ALU.add, ALU.is_equal))
                            own(e.tensor_scalar(gl[:, :], iotah[:, :], Ln[:, bass.ds(j, 1)], None, ALU.is_equal))
                            turn()
                        own(e.memset(gl[:, :], 0.0))
                        turn()
                        own(e.tensor_copy(cw[:, :, bass.ds(u * WD, WD)], pc[:, 0:WC].rearrange("p (d h) -> p h d", h=NT)))
                        own(e.tensor_scalar(base[:, :], base[:, :], float(WC), None, ALU.add))
                    for k in range(PL):
                        own(e.tensor_scalar(dg[:, :, :], cw[:, :, :], 8 * k, 255, ALU.logical_shift_right, ALU.bitwise_and))
                        hold(e, (s_w, w))
                        e.reg_add(w, w, 32)
                        own(e.tensor_scalar(pl[:, :, :], dg[:, :, :], 256.0 ** k, None, ALU.mult))
                        e.sem_inc(s_o, 1)
                        for g in range(7):
                            turn()
                            own(e.tensor_copy(plT[:, 7 * g:7 * g + 7, :], pt[:, 0:7 * P].rearrange("p (a n) -> p a n", a=7)))
                        e.sem_inc(s_o, 1)

        @b.tensor
        def _(e):
            e.wait_ge(s_c, 2)
            e.matmul(pf[0:1, 0:1], fv[:, :], onec[:, :], start=True, stop=True).then_inc(s_m, 1)
            go = flagged(e)
            n = e.alloc_register("gt_n")
            e.reg_mov(n, 1)

            def step():
                hold(e, (s_d, n))
                e.reg_add(n, n, 1)

            def count(start, stop):
                step()
                e.matmul(pc[:, 0:WC], gl[:, :], gk[:, :], start=start, stop=stop, skip_group_check=True).then_inc(s_p, 1)

            with e.If(go > 0):
                with e.Fori(0, NT) as t:
                    with e.Fori(0, WPT) as u:
                        c0, c1 = chunks(e, t, u)
                        count(True, False)
                        with e.Fori(c0, c1):
                            count(False, False)
                        count(False, True)
                    for k in range(PL):
                        for g in range(7):
                            step()
                            for i in range(7):
                                ins = e.transpose(pt[:, i * P:(i + 1) * P], pl[:, 7 * g + i, :], identb[:, :])
                            ins.then_inc(s_p, 1)

        @b.sync
        def _(e):
            e.sem_inc(s_w, 1)
            go = flagged(e)
            n = e.alloc_register("gs_n")
            e.reg_mov(n, 1)

            def step():
                hold(e, (s_o, n))
                e.reg_add(n, n, 1)

            with e.If(go > 0):
                with e.Fori(0, NT) as t:
                    for k in range(PL):
                        step()
                        e.dma_start(g_fwd[k, bass.ds(t, 1), :, :].rearrange("a p n -> p (a n)"),
                                    pl[:, :, :].rearrange("p s l -> p (s l)")).then_inc(s_w, 16)
                        step()
                        e.dma_start(g_bwd[k, :, :, bass.ds(t * P, P)].rearrange("s p l -> p s l"), plT[:, :, :]).then_inc(s_w, 16)
                e.wait_ge(s_w, 32 * PL * NT + 1)


class Lines:

    def __init__(self, sems):
        self.sems, self.n = sems, {k: 0 for k in sems}
        self.q = {k: [] for k in "vatgs"}

    def put(self, eng, make, *after):
        self.n[eng] += 1
        self.q[eng].append((make, after, True))
        return (self.sems[eng], self.n[eng])

    def raw(self, eng, make, *after):
        self.q[eng].append((make, after, False))

    def run(self, eng, e):
        for make, after, counted in self.q[eng]:
            for s, v in after:
                e.wait_ge(s, v)
            ins = make(e)
            if counted:
                ins.then_inc(self.sems[eng], 1)


def layers(nc, I, out, sem, sb, ps, V):
    X, S, ident, M = V["X"], V["S"], V["ident"], V["M"]
    a_fwd, a_bwd, g_fwd, g_bwd, flag = V["a_fwd"], V["a_bwd"], V["g_fwd"], V["g_bwd"], V["flag"]
    LAST = N - (NT - 1) * P
    with ExitStack() as C:
        Y = sb(C, "Y", [P, NT, D], F32)
        T = sb(C, "T", [P, NT, D], F32)
        U = sb(C, "U", [P, NT, D], F32)
        A = sb(C, "A", [P, NT, D], F32)
        R = sb(C, "R", [P, NT, D], F32)
        Z = sb(C, "Z", [P, NT, 3, D], BF16)
        slot = [sb(C, f"slot{r}", [P, NT * P], FP8) for r in range(NSLOT)]
        gslot = sb(C, "gslot", [P, NT * P], BF16)
        zb = sb(C, "zb", [P, P], BF16)
        tin = [sb(C, f"tin{r}", [D, 4, P], F32) for r in range(2)]
        cnt = sb(C, "cnt", [P, NT], F32)
        dv1 = sb(C, "dv1", [P, NT], F32)
        dv2 = sb(C, "dv2", [P, NT], F32)
        st = sb(C, "st", [P, 4, NT], F32)
        ones = sb(C, "ones", [P, P], F32)
        w0 = sb(C, "w0", [D, P], F32)
        w0t = sb(C, "w0t", [D, 2, D], F32)
        wmat = {n: sb(C, "m_" + n, [D, D], F32) for n in ("L1_gnn_W0", "L1_gnn_W1", "L1_gnn_W2", "L3_gnn_W1", "L3_gnn_W2")}
        rown = ["L0_gnn_b", "L3_gnn_b1", "L3_gnn_b2"] + [f"L1_gnn_{k}{i}" for k in ("b", "gamma", "beta") for i in range(3)]
        row = {n: sb(C, "r_" + n, [P, D], F32) for n in rown}
        bst = sb(C, "bst", [P, 4, D], F32)
        sc = sb(C, "sc", [P, 16], F32)
        p1 = sb(C, "p1", [32, D + 4], F32)
        p1t = sb(C, "p1t", [D, 32], F32)
        p2 = sb(C, "p2", [6, 32], F32)
        p2t = sb(C, "p2t", [32, 6], F32)
        pb1 = sb(C, "pb1", [32, 1], F32)
        pb2 = sb(C, "pb2", [P, 6], F32)
        hh = sb(C, "hh", [32, 8], F32)
        hb = sb(C, "hb", [32, P], F32)
        xm = sb(C, "xm", [D, 1], F32)
        co = sb(C, "co", [P, 3, 6], F32)
        bank = [ps(C, f"pc{i}", [P, 512], F32) for i in range(8)]
        s_w, s_out = sem("c_w"), sem("c_out")
        s_a = [sem(f"c_a{r}") for r in range(NSLOT)]
        s_pm, s_pr, s_fr = sem("c_pm"), sem("c_pr"), sem("c_fr")
        s_gl, s_gd = sem("c_gl"), sem("c_gd")
        L = Lines({k: sem("c_q" + k) for k in "vatg"})
        v = lambda f, *a: L.put("v", f, *a)
        a = lambda f, *w: L.put("a", f, *w)
        t = lambda f, *w: L.put("t", f, *w)

        def nb(ap):
            return ap.unsqueeze(2).to_broadcast([P, NT, D])

        def fb(ap):
            return ap.unsqueeze(1).to_broadcast([P, NT, D])

        def tt(o, x, y, op, *w):
            return v(lambda e: e.tensor_tensor(o, x, y, op), *w)

        def ts(o, x, s1, s2, o1, o2, *w):
            if o2 is None:
                return v(lambda e: e.tensor_scalar(o, x, s1, None, o1), *w)
            return v(lambda e: e.tensor_scalar(o, x, s1, s2, o1, o2), *w)

        def red(o, x, op, *w):
            return v(lambda e: e.tensor_reduce(o, x, AX.X, op), *w)

        def rsqrt(o, x, tmp, *w):
            k = a(lambda e: e.activation(tmp, x, ACT.Sqrt), *w)
            return v(lambda e: e.reciprocal(o, tmp), k)

        loads = []
        loads.append((w0[:, :], I["L0_gnn_W"]))
        for n, m in wmat.items():
            loads.append((m[:, :], I[n]))
        for n, m in row.items():
            loads.append((m[:, :], I[n].partition_broadcast(P)))
        loads.append((p1[:, :], I["L2_gnn_W1"]))
        loads.append((p2[:, :], I["L2_gnn_W2"]))
        loads.append((pb1[:, :], I["L2_gnn_b1"].rearrange("(p a) -> p a", a=1)))
        loads.append((pb2[:, :], I["L2_gnn_b2"].partition_broadcast(P)))
        for d, s in loads:
            L.raw("g", lambda e, d=d, s=s: e.dma_start(d, s).then_inc(s_w, 16))
        wl = (s_w, 16 * len(loads))

        npass = [0]
        regs, go = {}, {}

        def aggregate(src, back, *after):
            p = npass[0]
            npass[0] += 1
            k1 = v(lambda e: e.tensor_copy(Z[:, :, 0, :], src), *after)
            k2 = tt(T[:, :, :], src, Z[:, :, 0, :], ALU.subtract, k1)
            k3 = v(lambda e: e.tensor_copy(Z[:, :, 1, :], T[:, :, :]), k2)
            k4 = tt(Z[:, :, 2, :], T[:, :, :], Z[:, :, 1, :], ALU.subtract, k3)
            adj, gadj = (a_bwd, g_bwd) if back else (a_fwd, g_fwd)

            def load(e):
                with e.If(go["s"] < 1):
                    for c in range(NT):
                        e.wait_ge(s_fr, NT * p + c + 1)
                        e.dma_start(slot[c % NSLOT][:, :], adj[c]).then_inc(s_a[c % NSLOT], 16)
                with e.If(go["s"] > 0):
                    cd = regs["cd"]
                    with e.Fori(0, NT) as c:
                        for k in range(PL):
                            hold(e, (s_gd, cd))
                            e.reg_add(cd, cd, 1)
                            e.dma_start(gslot[:, :], gadj[k, bass.ds(c, 1), :, :].rearrange("a p n -> p (a n)")).then_inc(s_gl, 16)

            def mul(e):
                cp, ca, cg = regs["cp"], regs["ca"], regs["cg"]

                def tile(q, a, start, stop):
                    for c in range(NT):
                        ins = e.matmul(bank[q][:, 0:3 * D], a[:, c * P:(c + 1) * P],
                                       Z[:, c, :, :].rearrange("p a f -> p (a f)"), start=start and c == 0,
                                       stop=stop and c == NT - 1, skip_group_check=True)
                    return ins

                def nothing(q, start, stop):
                    return e.matmul(bank[q][:, 0:3 * D], zb[:, :], Z[:, 0, :, :].rearrange("p a f -> p (a f)"),
                                    start=start, stop=stop, skip_group_check=True)

                with e.If(go["t"] < 1):
                    e.reg_mov(cp, NT * p + 1)
                    e.reg_mov(ca, 16 * (7 * p + 1))
                    with e.Fori(0, 7):
                        for q in range(NSLOT):
                            hold(e, (s_pr, cp), (s_a[q], ca))
                            e.reg_add(cp, cp, 1)
                            tile(q, slot[q], True, True).then_inc(s_fr, 1)
                        e.reg_add(ca, ca, 16)
                with e.If(go["t"] > 0):
                    e.reg_mov(cp, NT * p + 1)
                    with e.Fori(0, 7):
                        for q in range(NSLOT):
                            hold(e, (s_pr, cp))
                            e.reg_add(cp, cp, 1)
                            nothing(q, True, False)
                            with e.Fori(0, PL):
                                hold(e, (s_gl, cg))
                                e.reg_add(cg, cg, 16)
                                tile(q, gslot, False, False).then_inc(s_gd, 1)
                            nothing(q, False, True).then_inc(s_fr, 1)

            def add(e):
                with e.Fori(0, 7) as i:
                    for q in range(NSLOT):
                        hold(e, (s_fr, 7 * i + (NT * p + q + 1 + NSLOT)))
                        e.tensor_reduce(A[:, bass.ds(i * 7 + q, 1), :].rearrange("p a f -> p (a f)"),
                                        bank[q][:, 0:3 * D].rearrange("p (a f) -> p f a", a=3), AX.X, ALU.add) \
                            .then_inc(s_pr, 1)

            L.raw("s", load)
            L.raw("t", mul, k4)
            L.raw("v", add)
            return (s_pr, 7 + NT * (p + 1))

        def project(dst, parts, *after):
            k = len(parts)
            copied, used, moved = [], [], []
            for gi, g in enumerate(range(0, NT, 4)):
                m = min(4, NT - g)
                o = bank[4 + gi % 2]
                got = []
                for src, w in parts:
                    i = len(copied)
                    pb, ti = bank[i % 2], tin[i % 2]
                    for c in range(m):
                        f = lambda e, pb=pb, src=src, c=c, g=g: e.transpose(pb[0:D, c * P:(c + 1) * P], src[:, g + c, :], ident[:, :])
                        tr = t(f, *after, *(copied[i - 2:i - 1] if i >= 2 else ()))
                    cp = a(lambda e, pb=pb, ti=ti, m=m: e.activation(ti[:, 0:m, :], pb[0:D, 0:m * P].rearrange("p (a n) -> p a n", n=P), ACT.Copy),
                           tr, *(used[(i - 2) // k:(i - 2) // k + 1] if i >= 2 else ()))
                    copied.append(cp)
                    got.append((ti, w))
                for c in range(m):
                    for j, (ti, w) in enumerate(got):
                        f = lambda e, o=o, c=c, ti=ti, w=w, j=j: e.matmul(o[:, c * D:(c + 1) * D], ti[:, c, :], w, start=(j == 0), stop=(j == k - 1))
                        mm = t(f, cp, *(moved[gi - 2:gi - 1] if gi >= 2 else ()))
                used.append(mm)
                last = v(lambda e, o=o, g=g, m=m: e.tensor_copy(dst[:, g:g + m, :], o[:, 0:m * D].rearrange("p (a f) -> p a f", f=D)), mm)
                moved.append(last)
            return last

        def layernorm(dst, y, *after):
            s, m, q, r = (st[:, i, :] for i in range(4))
            k = red(s, y, ALU.add, *after)
            k = ts(m, s, 1.0 / D, None, ALU.mult, None, k)
            k = tt(T[:, :, :], y, nb(m), ALU.subtract, k)
            k = a(lambda e: e.activation(U[:, :, :], T[:, :, :], ACT.Square), k)
            k = red(q, U[:, :, :], ALU.add, k)
            k = ts(q, q, 1.0 / D, EPS, ALU.mult, ALU.add, k)
            k = rsqrt(r, q, s, k)
            return tt(dst, T[:, :, :], nb(r), ALU.mult, k)

        def colsum(o, src, *after):
            for c in range(NT):
                lhs = ones[:, :] if c < NT - 1 else M[:, :]
                k = t(lambda e, c=c, lhs=lhs: e.matmul(o, lhs, src[:, c, :], start=(c == 0), stop=(c == NT - 1)), *(after if c == 0 else ()))
            return k

        x3, y3, t3, u3, a3, r3 = (m[:, :, :] for m in (X, Y, T, U, A, R))
        one = v(lambda e: e.memset(ones[:, :], 1.0))
        v(lambda e: e.memset(zb[:, :], 0.0))

        k = v(lambda e: e.tensor_copy(cnt[:, :], S[:, :, D]))
        kd = ts(dv1[:, :], cnt[:, :], 1.0, None, ALU.add, None, k)
        kd = rsqrt(dv1[:, :], dv1[:, :], st[:, 0, :], kd)
        ke = ts(dv2[:, :], cnt[:, :], 1e-12, None, ALU.max, None, kd)
        ke = rsqrt(dv2[:, :], dv2[:, :], st[:, 1, :], ke)
        k = ts(st[:, 2, :], cnt[:, :], 1.0, None, ALU.max, None, ke)
        k = v(lambda e: e.reciprocal(st[:, 3, :], st[:, 2, :]), k)
        kh = tt(r3, S[:, :, 0:D], nb(st[:, 3, :]), ALU.mult, k)
        for h in range(2):
            k = t(lambda e, h=h: e.transpose(bank[6][0:D, h * D:(h + 1) * D], w0[:, h * D:(h + 1) * D], ident[0:D, 0:D]), wl)
        k = v(lambda e: e.tensor_copy(w0t[:, :, :], bank[6][0:D, 0:2 * D].rearrange("p (a f) -> p a f", a=2)), k)
        k = project(Y, [(X, w0t[:, 0, :]), (R, w0t[:, 1, :])], k, kh)
        k = tt(y3, y3, x3, ALU.add, k)
        k = tt(y3, y3, fb(row["L0_gnn_b"][:, :]), ALU.add, k)
        kx = layernorm(x3, y3, k)

        src, k = x3, kx
        for i in range(3):
            k = tt(y3, src, nb(dv1[:, :]), ALU.mult, k)
            k2 = aggregate(y3, False, k)
            k = tt(a3, a3, y3, ALU.add, k2)
            k = tt(a3, a3, nb(dv1[:, :]), ALU.mult, k)
            k = project(R, [(A, wmat[f"L1_gnn_W{i}"][:, :])], k, wl)
            k = tt(r3, r3, fb(row[f"L1_gnn_b{i}"][:, :]), ALU.add, k)
            k = colsum(bank[6][:, 0:D], R, k, one)
            k = ts(bst[:, 0, :], bank[6][:, 0:D], 1.0 / N, None, ALU.mult, None, k)
            kc = tt(t3, r3, fb(bst[:, 0, :]), ALU.subtract, k)
            k = a(lambda e: e.activation(u3, t3, ACT.Square), kc)
            k = colsum(bank[6][:, D:2 * D], U, k)
            k = ts(bst[:, 1, :], bank[6][:, D:2 * D], 1.0 / N, EPS, ALU.mult, ALU.add, k)
            k = rsqrt(bst[:, 2, :], bst[:, 1, :], bst[:, 0, :], k)
            k = tt(bst[:, 3, :], bst[:, 2, :], row[f"L1_gnn_gamma{i}"][:, :], ALU.mult, k)
            k = tt(t3, t3, fb(bst[:, 3, :]), ALU.mult, k)
            k = tt(t3, t3, fb(row[f"L1_gnn_beta{i}"][:, :]), ALU.add, k)
            k = ts(u3, t3, 0.0, None, ALU.min, None, k)
            k = a(lambda e: e.activation(u3, u3, ACT.Exp), k)
            k = ts(t3, t3, 0.0, -1.0, ALU.max, ALU.add, k)
            k = tt(r3, t3, u3, ALU.add, k)
            src = r3
        k = tt(y3, x3, r3, ALU.add, k)
        kx = layernorm(x3, y3, k)

        k = colsum(bank[6][:, 0:D], X, kx)
        for c in range(NT):
            k = t(lambda e, c=c: e.matmul(bank[7][0:D, 0:1], X[:, c, :], (ones if c < NT - 1 else M)[:, 0:1], start=(c == 0), stop=(c == NT - 1)))
        km = ts(xm[:, :], bank[7][0:D, 0:1], 1.0 / N, None, ALU.mult, None, k)
        k = red(sc[:, 4:5], bank[6][:, 0:D], ALU.add, k)
        k = ts(sc[:, 0:1], sc[:, 4:5], 1.0 / (N * D), None, ALU.mult, None, k)
        k = ts(t3, x3, sc[:, 0:1], None, ALU.subtract, None, k)
        k = a(lambda e: e.activation(u3, t3, ACT.Square), k)
        k = colsum(bank[6][:, D:2 * D], U, k)
        k = red(sc[:, 5:6], bank[6][:, D:2 * D], ALU.add, k)
        k = ts(sc[:, 6:7], sc[:, 5:6], 1.0 / (N * D - 1), None, ALU.mult, None, k)
        k = a(lambda e: e.activation(sc[:, 1:2], sc[:, 6:7], ACT.Sqrt), k)
        v(lambda e: e.memset(sc[:, 2:3], float(N)))
        k3 = v(lambda e: e.memset(sc[:, 3:4], float(NE)))
        kt = t(lambda e: e.transpose(bank[7][0:D, 32:64], p1[:, 0:D], ident[0:32, 0:32]), wl, km)
        kt = t(lambda e: e.transpose(bank[7][0:32, 64:70], p2[:, :], ident[0:6, 0:6]))
        kq = v(lambda e: e.tensor_copy(p1t[:, :], bank[7][0:D, 32:64]), kt)
        kq = v(lambda e: e.tensor_copy(p2t[:, :], bank[7][0:32, 64:70]))
        kt = t(lambda e: e.matmul(bank[7][0:32, 80:81], p1t[:, :], xm[:, :], start=True, stop=True), kq)
        k = tt(hh[:, 0:4], p1[:, D:D + 4], sc[0:32, 0:4], ALU.mult, k, k3, wl)
        k = red(hh[:, 4:5], hh[:, 0:4], ALU.add, k)
        k = tt(hh[:, 5:6], hh[:, 4:5], pb1[:, :], ALU.add, k)
        k = tt(hh[:, 6:7], hh[:, 5:6], bank[7][0:32, 80:81], ALU.add, k, kt)
        k = ts(hh[:, 7:8], hh[:, 6:7], 0.0, None, ALU.max, None, k)
        k = ts(hb[:, :], ones[0:32, :], hh[:, 7:8], None, ALU.mult, None, k)
        k = t(lambda e: e.matmul(bank[7][:, 96:102], hb[:, :], p2t[:, :], start=True, stop=True), k)
        k = tt(co[:, 0, :], bank[7][:, 96:102], pb2[:, :], ALU.add, k)
        k = red(sc[:, 8:9], co[:, 0, :], ALU.max, k)
        k = ts(co[:, 1, :], co[:, 0, :], sc[:, 8:9], None, ALU.subtract, None, k)
        k = a(lambda e: e.activation(co[:, 1, :], co[:, 1, :], ACT.Exp), k)
        k = red(sc[:, 9:10], co[:, 1, :], ALU.add, k)
        k = v(lambda e: e.reciprocal(sc[:, 10:11], sc[:, 9:10]), k)
        k = ts(co[:, 2, :], co[:, 1, :], sc[:, 10:11], None, ALU.mult, None, k)
        kr = ts(r3, x3, co[:, 2, 0:1], None, ALU.mult, None, k)
        src, k = x3, kr
        for i in range(1, 6):
            k = tt(y3, src, nb(dv2[:, :]), ALU.mult, k)
            k = aggregate(y3, True, k)
            k = tt(a3, a3, nb(dv2[:, :]), ALU.mult, k)
            kr = v(lambda e, i=i: e.scalar_tensor_tensor(out=r3, in0=a3, scalar=co[:, 2, i:i + 1], in1=r3, op0=ALU.mult, op1=ALU.add), k)
            src, k = a3, kr
        k = tt(y3, x3, r3, ALU.add, k)
        kx = layernorm(x3, y3, k)

        k = aggregate(x3, False, kx)
        k = project(R, [(A, wmat["L3_gnn_W1"][:, :])], k)
        k = tt(r3, r3, fb(row["L3_gnn_b1"][:, :]), ALU.add, k)
        k = ts(r3, r3, 0.0, None, ALU.max, None, k)
        k = aggregate(r3, False, k)
        k = project(R, [(A, wmat["L3_gnn_W2"][:, :])], k)
        k = tt(r3, r3, fb(row["L3_gnn_b2"][:, :]), ALU.add, k)
        k = tt(y3, x3, r3, ALU.add, k)
        kx = layernorm(x3, y3, k)


        L.raw("s", lambda e: e.dma_start(out[0:(NT - 1) * P, :].rearrange("(t p) f -> p t f", p=P), X[:, 0:NT - 1, :]).then_inc(s_out, 16), kx)
        L.raw("s", lambda e: e.dma_start(out[(NT - 1) * P:N, :], X[0:LAST, NT - 1, :]).then_inc(s_out, 16))
        L.raw("s", lambda e: e.wait_ge(s_out, 32))

        b = C.enter_context(nc.Block())

        @b.sync
        def _(e):
            regs["cd"] = e.alloc_register("s_cd")
            e.reg_mov(regs["cd"], 1)
            e.sem_inc(s_gd, 1)
            go["s"] = values(nc, e, flag[0:1, 0:1])[0]
            L.run("s", e)

        @b.gpsimd
        def _(e):
            L.run("g", e)
            e.wait_ge(*wl)

        @b.scalar
        def _(e):
            L.run("a", e)

        @b.tensor
        def _(e):
            e.sem_inc(s_fr, NSLOT)
            for n in ("cp", "ca", "cg"):
                regs[n] = e.alloc_register("t_" + n)
            e.reg_mov(regs["cg"], 16)
            go["t"] = values(nc, e, flag[0:1, 0:1])[0]
            L.run("t", e)

        @b.vector
        def _(e):
            e.sem_inc(s_pr, 7)
            L.run("v", e)


_WEIGHTS = ["L0_gnn_W", "L0_gnn_b"] + [f"L1_gnn_{k}{i}" for i in range(3) for k in ("W", "b", "gamma", "beta")] + \
    [f"L{j}_gnn_{k}{i}" for j in (2, 3) for i in (1, 2) for k in ("W", "b")]


def kernel(**inputs):
    import numpy as _np
    import concourse.bacc as _bacc
    from concourse import mybir as _mybir
    from concourse.bass_utils import run_bass_kernel_spmd as _run

    def padded(a, n, fill):
        a = _np.asarray(a)
        return _np.concatenate([a, _np.full((n - a.shape[0],) + a.shape[1:], fill, a.dtype)])

    laid = {
        "x": padded(inputs["x"], NP_, 0),
        "src": padded(inputs["src"], NB * 512, 0).reshape(NB, 512),
        "dst": padded(inputs["dst"], NB * 512, 8191).reshape(NB, 512),
        "e": padded(inputs["edge_attr_64"], NB * 512, 0).reshape(NB, P, 4 * D),
    }
    for n in _WEIGHTS:
        laid[n] = _np.ascontiguousarray(inputs[n])
    nc = _bacc.Bacc("TRN2", target_bir_lowering=False, num_devices=1)
    arrays, args = {}, {}
    for n, v in laid.items():
        arrays[f"in_{n}"] = v
        args[n] = nc.dram_tensor(f"in_{n}", v.shape, _mybir.dt.from_np(v.dtype), kind="ExternalInput").ap()
    out = nc.dram_tensor("out_0", (N, D), F32, kind="ExternalOutput").ap()
    build(nc, args, out)
    r = _run(nc, [arrays], core_ids=[0])
    return r.results[0]["out_0"]
```

```python
from contextlib import ExitStack

import concourse.bass as bass
from concourse import mybir

F32 = mybir.dt.float32
F16 = mybir.dt.float16
BF16 = mybir.dt.bfloat16
FP8 = mybir.dt.float8e4
I32 = mybir.dt.int32
ALU = mybir.AluOpType
ACT = mybir.ActivationFunctionType
AX = mybir.AxisListType

P = 128
N = 6250
NE = 206250
D = 64
NT = 49
NP_ = NT * P
NB = 403
NC = NB * 4
WD = 8
WC = WD * NT
NW = NP_ // WD
WPT = P // WD
BPT = 8
RX = 12
RM = 3
NWS = 6
CH = 3
TG = 4
CAP = 16
PL = 3
QS = 4
NSLOT = 7
GT = 7
NG = NT // GT
EPS = 1e-5


def hold(eng, *pairs):
    vals = [(s, eng.snap(v)) for s, v in pairs]
    for s, v in vals:
        eng.wait_ge(s, v)


def values(nc, e, at):
    return nc.values_load_multi_w_load_instructions(
        at, engines=[e.engine], min_val=0, max_val=NC,
        skip_runtime_bounds_check_because="the tables hold chunk and tile numbers made on the chip")[1]


class Chain:

    def __init__(self, eng, sem):
        self.eng, self.sem, self.n = eng, sem, 0

    def op(self, ins):
        self.n += 1
        ins.then_inc(self.sem, 1)
        return (self.sem, self.n)

    def here(self):
        return (self.sem, self.n)

    def wait(self, *marks):
        for s, v in marks:
            self.eng.wait_ge(s, v)


def build(nc, I, out):
    with ExitStack() as G:
        def sb(ctx, name, shape, dt):
            return ctx.enter_context(nc.sbuf_tensor(name, shape, dt))

        def ps(ctx, name, shape, dt):
            return ctx.enter_context(nc.psum_tensor(name, shape, dt))

        def sem(name):
            return G.enter_context(nc.semaphore(name))

        a_fwd = nc.dram_tensor("a_fwd", (NT, P, NT * P), FP8).ap()
        a_bwd = nc.dram_tensor("a_bwd", (NT, P, NT * P), FP8).ap()
        g_fwd = nc.dram_tensor("g_fwd", (PL, NT, P, NT * P), BF16).ap()
        g_bwd = nc.dram_tensor("g_bwd", (PL, NT, P, NT * P), BF16).ap()
        d_win = nc.dram_tensor("d_win", (7, P, 2), I32).ap()
        d_blk = nc.dram_tensor("d_blk", (QS, P, 2), I32).ap()

        X = sb(G, "X", [P, NT, D], F32)
        S = sb(G, "S", [P, NT, D + 1], F32)
        ident = sb(G, "ident", [P, P], F32)
        identb = sb(G, "identb", [P, P], BF16)
        M = sb(G, "M", [P, P], F32)
        vio = sb(G, "vio", [P, NT, 7], F32)
        flag = sb(G, "flag", [1, 1], I32)

        AB = ExitStack()
        Kn = sb(AB, "Kn", [P, NC + 8], F32)
        Ln = sb(AB, "Ln", [P, NC + 8], F32)
        dstp = sb(AB, "dstp", [P, NB, 4], F32)
        srci = sb(AB, "srci", [P, NB, 4], I32)
        tabw = sb(AB, "tabw", [1, 7 * P * 2], I32)
        tabb = sb(AB, "tabb", [1, QS * P * 2], I32)
        iotaw = sb(AB, "iotaw", [P, WC], F16)
        iotap = sb(AB, "iotap", [P, P], F32)
        iotah = sb(AB, "iotah", [P, P], F16)
        ttab = sb(AB, "ttab", [P, NT], F32)
        xg = [sb(AB, f"xg{r}", [P, 4, D], F32) for r in range(RX)]
        s_x = [sem(f"b_x{r}") for r in range(RX)]

        prep(nc, I, sem, sb, ps, locals())
        edges(nc, I, sem, sb, ps, locals())
        planes(nc, sem, sb, ps, locals())
        AB.close()
        layers(nc, I, out, sem, sb, ps, locals())


def prep(nc, I, sem, sb, ps, V):
    Kn, Ln, dstp, srci = V["Kn"], V["Ln"], V["dstp"], V["srci"]
    ident, identb, M, X, S = V["ident"], V["identb"], V["M"], V["X"], V["S"]
    iotaw, iotap, iotah, ttab = V["iotaw"], V["iotap"], V["iotah"], V["ttab"]
    tabw, tabb, d_win, d_blk = V["tabw"], V["tabb"], V["d_win"], V["d_blk"]
    xg, s_g = V["xg"], V["s_x"]
    REG = [(P, slice(0, 3)), (NB - 3 * P, slice(3, 4))]
    with ExitStack() as C:
        src0 = sb(C, "src0", [P, RX, 4], I32)
        si = sb(C, "si", [P, QS, 512], I32)
        di = sb(C, "di", [P, QS, 512], I32)
        hi = sb(C, "hi", [P, QS, 512], I32)
        lo = sb(C, "lo", [P, QS, 512], I32)
        sf = sb(C, "sf", [P, QS, 512], F32)
        df = sb(C, "df", [P, QS, 512], F32)
        kf = sb(C, "kf", [P, QS, 512], F32)
        lf = sb(C, "lf", [P, QS, 512], F32)
        cmx = sb(C, "cmx", [P, QS, 4], F32)
        cmn = sb(C, "cmn", [P, QS, 4], F32)
        bmx = sb(C, "bmx", [P, QS], F32)
        bmn = sb(C, "bmn", [P, QS], F32)
        bi = sb(C, "bi", [P, QS, 2], I32)
        bj = sb(C, "bj", [P, QS, 2], I32)
        cxB = sb(C, "cxB", [P, NC], F32)
        cnB = sb(C, "cnB", [P, NC], F32)
        mk = sb(C, "mk", [P, NC], F32)
        m2 = sb(C, "m2", [P, NC], F32)
        itx = sb(C, "itx", [P, WC], I32)
        itp = sb(C, "itp", [P, P], I32)
        itt = sb(C, "itt", [P, NT], I32)
        itg = sb(C, "itg", [P, 7], I32)
        lo7 = sb(C, "lo7", [P, 7], F32)
        hi7 = sb(C, "hi7", [P, 7], F32)
        r1 = sb(C, "r1", [P, 7], F32)
        r0 = sb(C, "r0", [P, 7], F32)
        wi = sb(C, "wi", [P, 7, 2], I32)
        wf = sb(C, "wf", [P, 7, 2], F32)
        bank = [ps(C, f"pa{i}", [P, 512], F32) for i in range(4)]
        s_ld, s_gp, s_pe, s_v, s_a, s_tb, s_x, s_i = (sem(f"a_{n}") for n in ("ld", "gp", "pe", "v", "a", "tb", "x", "i"))

        b = C.enter_context(nc.Block())

        V_EDGE, V_BLK, V_WIN = [], [], []

        @b.vector
        def _(e):
            c = Chain(e, s_v)
            c.op(e.memset(S[:, :, :], 0.0))
            c.op(e.memset(Kn[:, NC:NC + 8], -1.0))
            c.op(e.memset(Ln[:, NC:NC + 8], -1.0))
            e.wait_ge(s_ld, 64)
            for k, q in REG:
                c.op(e.tensor_scalar(hi[0:k, q, :], si[0:k, q, :], 7, None, ALU.logical_shift_right))
                c.op(e.tensor_scalar(lo[0:k, q, :], si[0:k, q, :], 127, None, ALU.bitwise_and))
                c.op(e.tensor_copy(df[0:k, q, :], di[0:k, q, :]))
                c.op(e.tensor_copy(sf[0:k, q, :], si[0:k, q, :]))
            c.wait(c.here())
            for k, q in REG:
                c.op(e.scalar_tensor_tensor(out=kf[0:k, q, :], in0=df[0:k, q, :], scalar=float(NT),
                                            in1=hi[0:k, q, :], op0=ALU.mult, op1=ALU.add))
                c.op(e.tensor_copy(lf[0:k, q, :], lo[0:k, q, :]))
                d4 = df[0:k, q, :].rearrange("p q (m n) -> p q m n", m=4)
                c.op(e.tensor_reduce(cmx[0:k, q, :], d4, AX.X, ALU.max))
                c.op(e.tensor_reduce(cmn[0:k, q, :], d4, AX.X, ALU.min))
            V_EDGE.append(c.n)
            c.wait(c.here())
            for k, q in REG:
                c.op(e.tensor_reduce(bmx[0:k, q], cmx[0:k, q, :], AX.X, ALU.max))
                c.op(e.tensor_reduce(bmn[0:k, q], cmn[0:k, q, :], AX.X, ALU.min))
            c.wait(c.here())
            for k, q in REG:
                c.op(e.tensor_copy(bj[0:k, q, 0], bmn[0:k, q]))
                c.op(e.tensor_scalar(bj[0:k, q, 1], bmx[0:k, q], float(NP_ - 1), None, ALU.min))
            c.wait(c.here())
            for k, q in REG:
                c.op(e.tensor_scalar(bi[0:k, q, :], bj[0:k, q, :], 7, None, ALU.logical_shift_right))
            c.wait(c.here())
            for k, q in REG:
                c.op(e.tensor_scalar(bi[0:k, q, 1], bi[0:k, q, 1], 1.0, None, ALU.add))
            V_BLK.append(c.n)
            e.wait_ge(s_gp, 10)
            c.op(e.tensor_copy(iotaw[:, :], itx[:, :]))
            c.op(e.tensor_copy(iotap[:, :], itp[:, :]))
            c.op(e.tensor_copy(iotah[:, :], itp[:, :]))
            c.op(e.tensor_copy(ttab[:, :], itt[:, :]))
            c.op(e.tensor_copy(lo7[:, :], itg[:, :]))
            c.wait(c.here())
            c.op(e.tensor_scalar(hi7[:, :], lo7[:, :], float(WD - 1), None, ALU.add))
            c.wait(c.here())
            e.wait_ge(s_a, 24)
            c.op(e.tensor_tensor_scan(mk[:, :], cxB[:, :], cxB[:, :], 0.0, ALU.max, ALU.max))
            c.op(e.tensor_tensor_scan(m2[:, ::-1], cnB[:, ::-1], cnB[:, ::-1], 1e9, ALU.min, ALU.min))
            c.wait(c.here())
            for g in range(7):
                c.wait(c.here())
                c.op(e.tensor_scalar(cxB[:, :], mk[:, :], lo7[:, g:g + 1], 0.0, ALU.is_lt, ALU.add, accum_out=r0[:, g:g + 1]))
                c.op(e.tensor_scalar(cnB[:, :], m2[:, :], hi7[:, g:g + 1], 0.0, ALU.is_le, ALU.add, accum_out=r1[:, g:g + 1]))
            c.wait(c.here())
            c.op(e.tensor_scalar(wf[:, :, 0], r0[:, :], 1.0, None, ALU.add))
            c.wait(c.here())
            c.op(e.tensor_copy(wi[:, :, 0], r0[:, :]))
            c.op(e.tensor_tensor(wi[:, :, 1], r1[:, :], wf[:, :, 0], ALU.max))
            V_WIN.append(c.n)
            c.wait(c.here())

        @b.sync
        def _(e):
            e.dma_start(src0[:, :, :], I["src"][0:RX, :].rearrange("b (p m) -> p b m", m=4)).then_inc(s_i, 16)
            for dst, src in ((si, I["src"]), (di, I["dst"])):
                e.dma_start(dst[:, 0:3, :], src[0:3 * P, :].rearrange("(q p) n -> p q n", p=P)).then_inc(s_ld, 16)
                e.dma_start(dst[0:NB - 3 * P, 3, :], src[3 * P:NB, :]).then_inc(s_ld, 16)
            e.dma_start(X[:, :, :], I["x"].rearrange("(t p) f -> p t f", p=P)).then_inc(s_x, 16)
            e.wait_ge(s_v, V_BLK[0])
            for q in range(QS):
                n = min(P, NB - q * P)
                e.dma_start(d_blk[q, 0:n, :], bi[0:n, q, :]).then_inc(s_tb, 16)
            e.wait_ge(s_v, V_WIN[0])
            e.dma_start(d_win.rearrange("g p k -> p g k"), wi[:, :, :]).then_inc(s_tb, 16)
            e.wait_ge(s_tb, 16 * (QS + 1))
            e.dma_start(tabw[:, :], d_win.rearrange("g p k -> (g p k)").rearrange("(a n) -> a n", a=1)).then_inc(s_tb, 16)
            e.dma_start(tabb[:, 0:2 * NB], d_blk.rearrange("q p k -> (q p k)")[0:2 * NB].rearrange("(a n) -> a n", a=1)).then_inc(s_tb, 16)
            e.wait_ge(s_tb, 16 * (QS + 3))
            e.wait_ge(s_x, 16)

        @b.gpsimd
        def _(e):
            g = Chain(e, s_gp)
            g.op(e.memset(ident[:, :], 0.0))
            g.op(e.memset(identb[:, :], 0.0))
            g.op(e.memset(M[:, :], 1.0))
            g.wait(g.here())
            g.op(e.affine_select(out=ident[:, :], in_=ident[:, :], compare_op=ALU.not_equal, fill=1.0,
                                 base=0, pattern=[[-1, P]], channel_multiplier=1))
            g.op(e.affine_select(out=identb[:, :], in_=identb[:, :], compare_op=ALU.not_equal, fill=1.0,
                                 base=0, pattern=[[-1, P]], channel_multiplier=1))
            last = N - (NT - 1) * P
            g.op(e.affine_select(out=M[:, :], in_=M[:, :], compare_op=ALU.is_ge, fill=0.0,
                                 base=last - 1, pattern=[[0, P]], channel_multiplier=-1))
            g.op(e.iota(itx[:, :], pattern=[[1, WC]], base=0, channel_multiplier=0))
            g.op(e.iota(itp[:, :], pattern=[[1, P]], base=0, channel_multiplier=0))
            g.op(e.iota(itt[:, :], pattern=[[P, NT]], base=0, channel_multiplier=0))
            g.op(e.iota(itg[:, :], pattern=[[WD * P, 7]], base=0, channel_multiplier=WD))
            e.wait_ge(s_i, 16)
            for k in range(RX):
                for m in range(4):
                    e.indirect_dma_start(xg[k][:, m, :], None, I["x"],
                                         bass.IndirectOffsetOnAxis(ap=src0[:, k, m:m + 1], axis=0)) \
                        .then_inc(s_g[k], 16)

        tp = [(a, m) for a in range(4) for m in range(4)]
        rows = [(a, m) for a in range(2) for m in range(4)]

        @b.tensor
        def _(e):
            e.wait_ge(s_gp, 10)
            e.wait_ge(s_v, V_EDGE[0])
            n = 0
            for a, m in tp:
                if n >= 4:
                    e.wait_ge(s_a, n - 3)
                for q in range(QS):
                    k = min(P, NB - q * P)
                    src = (kf, lf, df, sf)[a]
                    v = src[0:k, q, m * P:(m + 1) * P] if a < 2 else src[0:k, q, m:512:4]
                    ins = e.transpose(bank[n % 4][:, q * P:q * P + k], v, ident[0:k, 0:k])
                ins.then_inc(s_pe, 1)
                n += 1
            for a, m in rows:
                e.wait_ge(s_a, n - 3)
                for q in range(QS):
                    k = min(P, NB - q * P)
                    c = (cmx, cmn)[a]
                    ins = e.matmul(bank[n % 4][:, q * P:q * P + k], c[0:k, q, m:m + 1].to_broadcast([k, P]),
                                   ident[0:k, 0:k], start=True, stop=True)
                ins.then_inc(s_pe, 1)
                n += 1

        @b.scalar
        def _(e):
            n = 0
            for a, m in tp:
                e.wait_ge(s_pe, n + 1)
                src = bank[n % 4][:, 0:NB]
                if a < 2:
                    d = (Kn, Ln)[a][:, 0:NC].rearrange("p (b m) -> p b m", m=4)[:, :, m]
                else:
                    d = (dstp, srci)[a - 2][:, :, m]
                e.activation(d, src, ACT.Copy).then_inc(s_a, 1)
                n += 1
            for a, m in rows:
                e.wait_ge(s_pe, n + 1)
                d = (cxB, cnB)[a][:, :].rearrange("p (b m) -> p b m", m=4)[:, :, m]
                e.activation(d, bank[n % 4][:, 0:NB], ACT.Copy).then_inc(s_a, 1)
                n += 1


def edges(nc, I, sem, sb, ps, V):
    Kn, Ln, dstp, srci = V["Kn"], V["Ln"], V["dstp"], V["srci"]
    ident, identb, S, vio = V["ident"], V["identb"], V["S"], V["vio"]
    iotaw, iotap, iotah, ttab = V["iotaw"], V["iotap"], V["iotah"], V["ttab"]
    tabw, tabb, a_fwd, a_bwd = V["tabw"], V["tabb"], V["a_fwd"], V["a_bwd"]
    xg, s_x = V["xg"], V["s_x"]
    with ExitStack() as C:
        eg = [sb(C, f"eg{r}", [P, 4 * D], F32) for r in range(RX)]
        msg = [sb(C, f"msg{r}", [P, 4, D + 1], F32) for r in range(RM)]
        oh = [sb(C, f"oh{r}", [P, 4, P], F32) for r in range(RM)]
        ohx = sb(C, "ohx", [P, 4, P], F32)
        wk = [sb(C, f"wk{r}", [P, CH, WC], BF16) for r in range(NWS)]
        wl = [sb(C, f"wl{r}", [P, CH, P], BF16) for r in range(NWS)]
        wkx = sb(C, "wkx", [P, CH, WC], BF16)
        wlx = sb(C, "wlx", [P, CH, P], BF16)
        stage = sb(C, "stage", [P, 2, NT, P], BF16)
        stg8 = sb(C, "stg8", [P, 2, NT * P], FP8)
        stgT = sb(C, "stgT", [P, NT, TG * P], FP8)
        junk = sb(C, "junk", [P, 2, 7 * P], FP8)
        ncap = sb(C, "ncap", [P, 1], F32)
        pw = [ps(C, f"pw{r}", [P, 512], F32) for r in range(3)]
        pm = [ps(C, f"pm{r}", [P, 512], F32) for r in range(2)]
        pmx = ps(C, "pmx", [P, 512], F32)
        pt = [ps(C, f"pt{r}", [P, 1024], BF16) for r in range(2)]
        s_e = [sem(f"b_e{r}") for r in range(RX)]
        s_use, s_one = sem("b_use"), sem("b_one")
        s_oh, s_mm, s_sv = sem("b_oh"), sem("b_mm"), sem("b_sv")
        s_oy, s_my, s_sy = sem("b_oy"), sem("b_my"), sem("b_sy")
        s_wo, s_wm, s_wv = sem("b_wo"), sem("b_wm"), sem("b_wv")
        s_xo, s_xm = sem("b_xo"), sem("b_xm")
        s_tt, s_te, s_c8 = sem("b_tt"), sem("b_te"), sem("b_c8")
        s_af, s_ab, s_jk = sem("b_af"), sem("b_ab"), sem("b_jk")

        def tiles(e, k):
            t0, t1 = values(nc, e, tabb[0:1, 2 * k:2 * k + 2])
            return t0.with_bounds(min_val=0, max_val=NT - 1), t1.with_bounds(min_val=1, max_val=NT)

        def pairs(e, k):
            v = values(nc, e, tabw[0:1, 4 * k:4 * k + 4])
            return [(v[2 * i].with_bounds(min_val=0, max_val=NC), v[2 * i + 1].with_bounds(min_val=1, max_val=NC + 1)) for i in range(2)]

        def side(t, u):
            return (t - 1, u - 1) if 1 <= t <= NT and 1 <= u <= 7 else None

        b = C.enter_context(nc.Block())

        @b.sync
        def _(e):
            for k in range(NB):
                if k >= RX:
                    e.wait_ge(s_use, k - RX + 1)
                e.dma_start(eg[k % RX][:, :], I["e"][k]).then_inc(s_e[k % RX], 16)
                t, u = divmod(k, BPT)
                if u == 1 and 2 <= t <= NT + 1:
                    e.wait_ge(s_c8, 7 * (t - 1))
                    e.dma_start(a_fwd[t - 2], stg8[:, t % 2, :]).then_inc(s_af, 16)
                if (u == 2 and t >= 2 and (t - 1) % TG == 0) or k == NB - 1:
                    q = (t - 2) // TG if k < NB - 1 else (NT - 1) // TG
                    n = min(TG, NT - TG * q)
                    e.wait_ge(s_te, 7 * (TG * q + n))
                    e.dma_start(a_bwd[:, :, TG * q * P:(TG * q + n) * P].rearrange("s p l -> p s l"),
                                stgT[:, :, 0:n * P]).then_inc(s_ab, 16)
            e.wait_ge(s_af, 16 * NT)
            e.wait_ge(s_ab, 16 * ((NT + TG - 1) // TG))

        @b.gpsimd
        def _(e):
            for k in range(RX, NB):
                e.wait_ge(s_use, k - RX + 1)
                for m in range(4):
                    e.indirect_dma_start(xg[k % RX][:, m, :], None, I["x"],
                                         bass.IndirectOffsetOnAxis(ap=srci[:, k, m:m + 1], axis=0)) \
                        .then_inc(s_x[k % RX], 16)

        @b.vector
        def _(e):
            for r in range(RM):
                e.memset(msg[r][:, :, D:D + 1], 1.0).then_inc(s_one, 1)
            e.memset(ncap[:, :], -float(CAP)).then_inc(s_one, 1)
            cy, cx = e.alloc_register("v_cy"), e.alloc_register("v_cx")
            e.reg_mov(cy, 1)
            e.reg_mov(cx, 1)

            def hits(o, k, tile):
                return e.scalar_tensor_tensor(out=o[:, :, :], in0=iotap[:, :].unsqueeze(1).to_broadcast([P, 4, P]),
                                              scalar=ttab[:, bass.ds(tile, 1)],
                                              in1=dstp[:, k, :].unsqueeze(2).to_broadcast([P, 4, P]),
                                              op0=ALU.add, op1=ALU.is_equal)

            def block(k):
                r, h = k % RX, k % RM
                t0, t1 = tiles(e, k)
                e.wait_ge(s_x[r], 64 * (k // RX + 1))
                e.wait_ge(s_e[r], 16 * (k // RX + 1))
                if k >= RM:
                    e.wait_ge(s_mm, k - RM + 1)
                e.tensor_tensor(msg[h][:, :, 0:D], xg[r][:, :, :], eg[r][:, :].rearrange("p (m f) -> p m f", m=4),
                                ALU.mult).then_inc(s_use, 1)
                with e.If(t0 + 1 < t1):
                    with e.Fori(t0 + 1, t1) as j:
                        hold(e, (s_my, cy))
                        hits(ohx, k, j).then_inc(s_oy, 1)
                        e.reg_add(cy, cy, 1)
                hits(oh[h], k, t0).then_inc(s_oh, 1)

            def marks(o, l, w, c):
                e.tensor_tensor(l[:, :, :], iotah[:, :].unsqueeze(1).to_broadcast([P, CH, P]),
                                Ln[:, bass.ds(c, CH)].unsqueeze(2).to_broadcast([P, CH, P]), ALU.is_equal)
                for m in range(CH):
                    ins = e.tensor_scalar(o[:, m, :], iotaw[:, :], float(WC * w), Kn[:, bass.ds(c + m, 1)],
                                          ALU.add, ALU.is_equal)
                return ins

            def window(w, c0, c1):
                if w >= NWS:
                    e.wait_ge(s_wm, w - NWS + 1)
                marks(wk[w % NWS], wl[w % NWS], w, c0).then_inc(s_wo, 1)
                with e.If(c0 + CH < c1):
                    with e.Fori(c0 + CH, c1, CH) as j:
                        hold(e, (s_xm, cx))
                        marks(wkx, wlx, w, j).then_inc(s_xo, 1)
                        e.reg_add(cx, cx, 1)

            for k in range(NB):
                block(k)
                if 2 * k < NW:
                    for i, c in enumerate(pairs(e, k)):
                        window(2 * k + i, *c)

        @b.tensor
        def _(e):
            e.wait_ge(s_one, RM + 1)
            e.sem_inc(s_xm, 1)
            e.sem_inc(s_my, 1)
            cy, cx = e.alloc_register("t_cy"), e.alloc_register("t_cx")
            e.reg_mov(cy, 1)
            e.reg_mov(cx, 1)

            def gather(o, k, tile, hot):
                e.matmul(o[:, 0:D + 1], ident[:, :], S[:, bass.ds(tile, 1), :], start=True, stop=False)
                for m in range(4):
                    ins = e.matmul(o[:, 0:D + 1], hot[:, m, :], msg[k % RM][:, m, :], start=False, stop=(m == 3))
                return ins

            def block(k):
                t0, t1 = tiles(e, k)
                if k >= 1:
                    e.wait_ge(s_sv, k)
                with e.If(t0 + 1 < t1):
                    with e.Fori(t0 + 1, t1) as j:
                        hold(e, (s_sy, cy), (s_oy, cy))
                        gather(pmx, k, j, ohx).then_inc(s_my, 1)
                        e.reg_add(cy, cy, 1)
                e.wait_ge(s_oh, k + 1)
                gather(pm[k % 2], k, t0, oh[k % RM]).then_inc(s_mm, 1)

            def window(w, c0, c1):
                o = pw[w % 3][:, 0:WC]
                k, l = wk[w % NWS], wl[w % NWS]
                e.wait_ge(s_wo, w + 1)
                if w >= 3:
                    e.wait_ge(s_wv, w - 2)
                for m in range(CH - 1):
                    e.matmul(o, l[:, m, :], k[:, m, :], start=(m == 0), stop=False, skip_group_check=True)
                with e.If(c0 + CH < c1):
                    with e.Fori(c0 + CH, c1, CH):
                        hold(e, (s_xo, cx))
                        for m in range(CH):
                            ins = e.matmul(o, wlx[:, m, :], wkx[:, m, :], start=False, stop=False, skip_group_check=True)
                        ins.then_inc(s_xm, 1)
                        e.reg_add(cx, cx, 1)
                e.matmul(o, l[:, CH - 1, :], k[:, CH - 1, :], start=False, stop=True, skip_group_check=True).then_inc(s_wm, 1)

            def turn(t, g):
                n = 7 * t + g
                if g == 0:
                    e.wait_ge(s_wv, WPT * (t + 1))
                if n >= 2:
                    e.wait_ge(s_te, n - 1)
                for m in range(7):
                    ins = e.transpose(pt[n % 2][:, m * P:(m + 1) * P], stage[:, t % 2, 7 * g + m, :], identb[:, :])
                ins.then_inc(s_tt, 1)

            for k in range(NB):
                block(k)
                if 2 * k < NW:
                    for i, c in enumerate(pairs(e, k)):
                        window(2 * k + i, *c)
                if side(*divmod(k, BPT)):
                    turn(*side(*divmod(k, BPT)))

        @b.scalar
        def _(e):
            e.sem_inc(s_sy, 1)
            e.wait_ge(s_one, RM + 1)
            cy = e.alloc_register("a_cy")
            e.reg_mov(cy, 2)

            def block(k):
                t0, t1 = tiles(e, k)
                with e.If(t0 + 1 < t1):
                    with e.Fori(t0 + 1, t1) as j:
                        hold(e, (s_my, cy))
                        e.activation(S[:, bass.ds(j, 1), :], pmx[:, 0:D + 1], ACT.Copy).then_inc(s_sy, 1)
                        e.reg_add(cy, cy, 1)
                e.wait_ge(s_mm, k + 1)
                e.activation(S[:, bass.ds(t0, 1), :], pm[k % 2][:, 0:D + 1], ACT.Copy).then_inc(s_sv, 1)

            def window(w):
                t, u = divmod(w, WPT)
                if u == 0 and t >= 2:
                    e.wait_ge(s_jk, 7 * (t - 1))
                e.wait_ge(s_wm, w + 1)
                e.activation(stage[:, t % 2, :, u * WD:(u + 1) * WD],
                             pw[w % 3][:, 0:WC].rearrange("p (d h) -> p h d", h=NT), ACT.Copy).then_inc(s_wv, 1)

            def turned(t, g):
                n = 7 * t + g
                flat = stage[:, t % 2, 7 * g:7 * g + 7, :].rearrange("p s l -> p (s l)")
                if g == 0:
                    e.wait_ge(s_wv, WPT * (t + 1))
                    if t % TG == 0 and t:
                        e.wait_ge(s_ab, 16 * (t // TG))
                    if t >= 2:
                        e.wait_ge(s_af, 16 * (t - 1))
                e.activation(stg8[:, t % 2, 7 * g * P:7 * (g + 1) * P], flat, ACT.Copy, saturate=False).then_inc(s_c8, 1)
                if n >= 2:
                    e.wait_ge(s_jk, n - 1)
                e.activation(junk[:, n % 2, :], flat, ACT.Relu, bias=ncap[:, :], accum_out=vio[:, t, g:g + 1],
                             saturate=False).then_inc(s_jk, 1)
                e.wait_ge(s_tt, n + 1)
                e.activation(stgT[:, 7 * g:7 * g + 7, (t % TG) * P:(t % TG + 1) * P],
                             pt[n % 2][:, 0:7 * P].rearrange("p (a n) -> p a n", a=7), ACT.Copy,
                             saturate=False).then_inc(s_te, 1)

            for k in range(NB):
                block(k)
                if 2 * k < NW:
                    window(2 * k)
                    window(2 * k + 1)
                if side(*divmod(k, BPT)):
                    turned(*side(*divmod(k, BPT)))


def planes(nc, sem, sb, ps, V):
    Kn, Ln, iotaw, iotah, tabw = V["Kn"], V["Ln"], V["iotaw"], V["iotah"], V["tabw"]
    identb, vio, flag, g_fwd, g_bwd = V["identb"], V["vio"], V["flag"], V["g_fwd"], V["g_bwd"]
    with ExitStack() as C:
        fv = sb(C, "fv", [P, 1], F32)
        onec = sb(C, "onec", [P, 1], F32)
        base = sb(C, "base", [P, 1], F32)
        gk = sb(C, "gk", [P, WC], BF16)
        gl = sb(C, "gl", [P, P], BF16)
        cw = sb(C, "cw", [P, NT, P], I32)
        dg = sb(C, "dg", [P, NT, P], I32)
        pl = sb(C, "pl", [P, NT, P], BF16)
        plT = sb(C, "plT", [P, NT, P], BF16)
        pf = ps(C, "pf", [P, 512], F32)
        pc = ps(C, "pcw", [P, 512], F32)
        pt = ps(C, "ptg", [P, 1024], BF16)
        s_c, s_f, s_m = sem("g_c"), sem("g_f"), sem("g_m")
        s_own, s_d, s_p, s_o, s_w = (sem(f"g_{n}") for n in ("own", "d", "p", "o", "w"))

        b = C.enter_context(nc.Block())

        def flagged(e):
            e.wait_ge(s_f, 1)
            return values(nc, e, flag[0:1, 0:1])[0]

        def chunks(e, t, u):
            c0, c1 = values(nc, e, tabw[0:1, bass.ds((t * WPT + u) * 2, 2)])
            return c0.with_bounds(min_val=0, max_val=NC - 1), c1.with_bounds(min_val=1, max_val=NC)

        @b.vector
        def _(e):
            c = Chain(e, s_c)
            c.op(e.memset(onec[:, :], 1.0))
            c.op(e.tensor_reduce(fv[:, :], vio[:, :, :].rearrange("p t g -> p (t g)"), AX.X, ALU.add))
            e.wait_ge(s_m, 1)
            e.tensor_scalar(flag[0:1, 0:1], pf[0:1, 0:1], 1.0, None, ALU.min).then_inc(s_f, 1)
            go = flagged(e)
            n, m, w = (e.alloc_register("gv_" + x) for x in "nmw")
            for r in (n, m, w):
                e.reg_mov(r, 1)

            def own(ins):
                ins.then_inc(s_own, 1)
                hold(e, (s_own, m))
                e.reg_add(m, m, 1)

            def turn():
                e.sem_inc(s_d, 1)
                hold(e, (s_p, n))
                e.reg_add(n, n, 1)

            with e.If(go > 0):
                own(e.memset(base[:, :], 0.0))
                own(e.memset(gk[:, :], 0.0))
                with e.Fori(0, NT) as t:
                    with e.Fori(0, WPT) as u:
                        c0, c1 = chunks(e, t, u)
                        own(e.memset(gl[:, :], 0.0))
                        turn()
                        with e.Fori(c0, c1) as j:
                            own(e.tensor_scalar(gk[:, :], iotaw[:, :], base[:, :], Kn[:, bass.ds(j, 1)], ALU.add, ALU.is_equal))
                            own(e.tensor_scalar(gl[:, :], iotah[:, :], Ln[:, bass.ds(j, 1)], None, ALU.is_equal))
                            turn()
                        own(e.memset(gl[:, :], 0.0))
                        turn()
                        own(e.tensor_copy(cw[:, :, bass.ds(u * WD, WD)], pc[:, 0:WC].rearrange("p (d h) -> p h d", h=NT)))
                        own(e.tensor_scalar(base[:, :], base[:, :], float(WC), None, ALU.add))
                    for k in range(PL):
                        own(e.tensor_scalar(dg[:, :, :], cw[:, :, :], 8 * k, 255, ALU.logical_shift_right, ALU.bitwise_and))
                        hold(e, (s_w, w))
                        e.reg_add(w, w, 32)
                        own(e.tensor_scalar(pl[:, :, :], dg[:, :, :], 256.0 ** k, None, ALU.mult))
                        e.sem_inc(s_o, 1)
                        for g in range(7):
                            turn()
                            own(e.tensor_copy(plT[:, 7 * g:7 * g + 7, :], pt[:, 0:7 * P].rearrange("p (a n) -> p a n", a=7)))
                        e.sem_inc(s_o, 1)

        @b.tensor
        def _(e):
            e.wait_ge(s_c, 2)
            e.matmul(pf[0:1, 0:1], fv[:, :], onec[:, :], start=True, stop=True).then_inc(s_m, 1)
            go = flagged(e)
            n = e.alloc_register("gt_n")
            e.reg_mov(n, 1)

            def step():
                hold(e, (s_d, n))
                e.reg_add(n, n, 1)

            def count(start, stop):
                step()
                e.matmul(pc[:, 0:WC], gl[:, :], gk[:, :], start=start, stop=stop, skip_group_check=True).then_inc(s_p, 1)

            with e.If(go > 0):
                with e.Fori(0, NT) as t:
                    with e.Fori(0, WPT) as u:
                        c0, c1 = chunks(e, t, u)
                        count(True, False)
                        with e.Fori(c0, c1):
                            count(False, False)
                        count(False, True)
                    for k in range(PL):
                        for g in range(7):
                            step()
                            for i in range(7):
                                ins = e.transpose(pt[:, i * P:(i + 1) * P], pl[:, 7 * g + i, :], identb[:, :])
                            ins.then_inc(s_p, 1)

        @b.sync
        def _(e):
            e.sem_inc(s_w, 1)
            go = flagged(e)
            n = e.alloc_register("gs_n")
            e.reg_mov(n, 1)

            def step():
                hold(e, (s_o, n))
                e.reg_add(n, n, 1)

            with e.If(go > 0):
                with e.Fori(0, NT) as t:
                    for k in range(PL):
                        step()
                        e.dma_start(g_fwd[k, bass.ds(t, 1), :, :].rearrange("a p n -> p (a n)"),
                                    pl[:, :, :].rearrange("p s l -> p (s l)")).then_inc(s_w, 16)
                        step()
                        e.dma_start(g_bwd[k, :, :, bass.ds(t * P, P)].rearrange("s p l -> p s l"), plT[:, :, :]).then_inc(s_w, 16)
                e.wait_ge(s_w, 32 * PL * NT + 1)


class Lines:

    def __init__(self, sems):
        self.sems, self.n = sems, {k: 0 for k in sems}
        self.q = {k: [] for k in "vatgs"}

    def put(self, eng, make, *after):
        self.n[eng] += 1
        self.q[eng].append((make, after, True))
        return (self.sems[eng], self.n[eng])

    def raw(self, eng, make, *after):
        self.q[eng].append((make, after, False))

    def run(self, eng, e, exact):
        for make, after, counted in self.q[eng]:
            for s, v in after:
                e.wait_ge(s, v)
            if counted:
                make(e).then_inc(self.sems[eng], 1)
            else:
                make(e, exact)


def layers(nc, I, out, sem, sb, ps, V):
    X, S, ident, M = V["X"], V["S"], V["ident"], V["M"]
    a_fwd, a_bwd, g_fwd, g_bwd, flag = V["a_fwd"], V["a_bwd"], V["g_fwd"], V["g_bwd"], V["flag"]
    LAST = N - (NT - 1) * P
    with ExitStack() as C:
        Y, A, R = (sb(C, n, [P, NT, D], F32) for n in "YAR")
        TU = sb(C, "TU", [P, NT, 2 * D], F32)
        T, U = TU[:, :, 0:D], TU[:, :, D:2 * D]
        Z = [sb(C, f"Z{r}", [P, NT, 3, D], BF16) for r in range(2)]
        slot = [sb(C, f"slot{r}", [P, NT * P], FP8) for r in range(NSLOT)]
        zb = sb(C, "zb", [P, P], BF16)
        tin = [sb(C, f"tin{r}", [P, GT, P], F32) for r in range(2)]
        cnt = sb(C, "cnt", [P, NT], F32)
        inv = sb(C, "inv", [P, NT], F32)
        dv1 = sb(C, "dv1", [P, NT], F32)
        dv2 = sb(C, "dv2", [P, NT], F32)
        st = sb(C, "st", [P, 5, NT], F32)
        ones = sb(C, "ones", [P, P], F32)
        w0 = sb(C, "w0", [D, P], F32)
        w0t = sb(C, "w0t", [P, D], F32)
        wmat = {n: sb(C, "m_" + n, [D, D], F32) for n in ("L1_gnn_W0", "L1_gnn_W1", "L1_gnn_W2", "L3_gnn_W1", "L3_gnn_W2")}
        rown = ["L0_gnn_b", "L3_gnn_b1", "L3_gnn_b2"] + [f"L1_gnn_{k}{i}" for k in ("b", "gamma", "beta") for i in range(3)]
        row = {n: sb(C, "r_" + n, [P, D], F32) for n in rown}
        bst = sb(C, "bst", [P, 4, D], F32)
        cs = sb(C, "cs", [P, NG, D], F32)
        sc = sb(C, "sc", [P, 16], F32)
        p1 = sb(C, "p1", [32, D + 4], F32)
        p1t = sb(C, "p1t", [D, 32], F32)
        p2 = sb(C, "p2", [6, 32], F32)
        p2t = sb(C, "p2t", [32, 6], F32)
        pb1 = sb(C, "pb1", [32, 1], F32)
        pb2 = sb(C, "pb2", [P, 6], F32)
        hh = sb(C, "hh", [32, 8], F32)
        hb = sb(C, "hb", [32, P], F32)
        xm = sb(C, "xm", [D, 1], F32)
        co = sb(C, "co", [P, 3, 6], F32)
        bank = [ps(C, f"pc{i}", [P, 512], F32) for i in range(8)]
        s_w, s_w0, s_out = sem("c_w"), sem("c_w0"), sem("c_out")
        s_a = [sem(f"c_a{r}") for r in range(NSLOT)]
        s_pr, s_fr, s_gl, s_gd = sem("c_pr"), sem("c_fr"), sem("c_gl"), sem("c_gd")
        gslot = S[:, :, :].rearrange("p t f -> p (t f)").bitcast(BF16)[:, 0:NT * P]
        regs = {}
        L = Lines({k: sem("c_q" + k) for k in "vatg"})
        v = lambda f, *w: L.put("v", f, *w)
        a = lambda f, *w: L.put("a", f, *w)
        t = lambda f, *w: L.put("t", f, *w)

        def gr(m, g):
            return m[:, g * GT:(g + 1) * GT, :]

        def gs(m, g):
            return m[:, g * GT:(g + 1) * GT]

        def nb(m, g):
            return gs(m, g).unsqueeze(2).to_broadcast([P, GT, D])

        def fb(m):
            return m.unsqueeze(1).to_broadcast([P, GT, D])

        def tt(o, x, y, op, *w, eng="v"):
            return L.put(eng, lambda e: e.tensor_tensor(o, x, y, op), *w)

        def ts(o, x, s1, s2, o1, o2, *w):
            if o2 is None:
                return v(lambda e: e.tensor_scalar(o, x, s1, None, o1), *w)
            return v(lambda e: e.tensor_scalar(o, x, s1, s2, o1, o2), *w)

        def stt(o, x, s, y, o1, o2, *w):
            return v(lambda e: e.scalar_tensor_tensor(out=o, in0=x, scalar=s, in1=y, op0=o1, op1=o2), *w)

        def red(o, x, op, *w):
            return v(lambda e: e.tensor_reduce(o, x, AX.X, op), *w)

        def act(o, x, fn, *w, scale=1.0):
            return a(lambda e: e.activation(o, x, fn, scale=scale), *w)

        def rsqrt(o, x, tmp, *w):
            k = act(tmp, x, ACT.Sqrt, *w)
            return v(lambda e: e.reciprocal(o, tmp), k)

        def pipe(*stages):
            got = [dict() for _ in stages]
            for n in range(NG + len(stages) - 1):
                for j, f in reversed(list(enumerate(stages))):
                    g = n - j
                    if 0 <= g < NG:
                        got[j][g] = f(g, got[j - 1][g] if j else ())
            return got[-1]

        soon = [(w0[:, :], I["L0_gnn_W"]), (row["L0_gnn_b"][:, :], I["L0_gnn_b"].partition_broadcast(P))]
        loads = [(m[:, :], I[n]) for n, m in wmat.items()]
        loads += [(m[:, :], I[n].partition_broadcast(P)) for n, m in row.items() if n != "L0_gnn_b"]
        loads += [(p1[:, :], I["L2_gnn_W1"]), (p2[:, :], I["L2_gnn_W2"]),
                  (pb1[:, :], I["L2_gnn_b1"].rearrange("(p a) -> p a", a=1)),
                  (pb2[:, :], I["L2_gnn_b2"].partition_broadcast(P))]
        for d, s in soon:
            L.raw("s", lambda e, x, d=d, s=s: e.dma_start(d, s).then_inc(s_w0, 16))
        for d, s in loads:
            L.raw("s", lambda e, x, d=d, s=s: e.dma_start(d, s).then_inc(s_w, 16))
        wl, w0l = (s_w, 16 * len(loads)), (s_w0, 16 * len(soon))

        def split0(z, g, src, *w):
            return act(z[:, g * GT:(g + 1) * GT, 0, :], src, ACT.Copy, *w)

        def split1(z, g, src, *w):
            k = tt(gr(T, g), src, z[:, g * GT:(g + 1) * GT, 0, :], ALU.subtract, *w)
            return act(z[:, g * GT:(g + 1) * GT, 1, :], gr(T, g), ACT.Copy, k)

        def split2(z, g, *w):
            return tt(z[:, g * GT:(g + 1) * GT, 2, :], gr(T, g), z[:, g * GT:(g + 1) * GT, 1, :], ALU.subtract, *w)

        def split(z, g, src, *w):
            return split2(z, g, split1(z, g, src, split0(z, g, src, *w), *w))

        class Project:

            def __init__(self, src, n, weight, use, loaded):
                self.src, self.n, self.weight, self.use, self.loaded = src, n, weight, use, loaded
                self.cp, self.mm, self.done = {}, {}, {}

            def turn(self, g, *w):
                self.cp[g] = []
                n, src = self.n, self.src
                for h, (c0, c1) in enumerate(((0, 4), (4, GT))):
                    o = bank[4 + h]
                    prev = (self.cp[g - 1][h],) if g else ()
                    for c in range(c0, c1):
                        k = t(lambda e, o=o, c=c, c0=c0: e.transpose(o[0:n, (c - c0) * P:(c - c0 + 1) * P],
                                                                    src[:, g * GT + c, :], ident[:, :]), *w, *prev)
                    used = (self.mm[g - 2],) if g >= 2 else ()
                    self.cp[g].append(act(tin[g % 2][0:n, c0:c1, :], o[0:n, 0:(c1 - c0) * P].rearrange("p (a n) -> p a n", n=P),
                                          ACT.Copy, k, *used))

            def late(self, g):
                for c in range(GT):
                    k = t(lambda e, c=c: e.matmul(bank[6][:, c * D:(c + 1) * D], tin[g % 2][0:self.n, c, :], self.weight,
                                                 start=True, stop=True),
                          *self.cp[g], self.loaded, *((self.done[g - 1],) if g else ()))
                self.mm[g] = k
                self.done[g], r = self.use(g, bank[6][:, 0:GT * D].rearrange("p (a f) -> p a f", f=D), k)
                return r

        npass = [0]

        def sweep(z, zm, back, ready, proj=None, before=None, extra=None, start=()):
            p = npass[0]
            npass[0] += 1
            adj, gadj = (a_bwd, g_bwd) if back else (a_fwd, g_fwd)

            def load(e, exact):
                if exact:
                    for s, n in start:
                        e.wait_ge(s, n)
                    with e.Fori(0, NT) as c:
                        for k in range(PL):
                            hold(e, (s_gd, regs["cd"]))
                            e.reg_add(regs["cd"], regs["cd"], 1)
                            e.dma_start(gslot, gadj[k, bass.ds(c, 1), :, :].rearrange("a p n -> p (a n)")).then_inc(s_gl, 16)
                    return
                for c in range(NT):
                    n = NT * p + c
                    if n >= NSLOT:
                        e.wait_ge(s_fr, n - NSLOT + 1)
                    e.dma_start(slot[n % NSLOT][:, :], adj[c]).then_inc(s_a[n % NSLOT], 16)

            def product(e, n, a8, c, s, f):
                return e.matmul(bank[n % 4][:, 0:3 * D], a8, z[:, c, :, :].rearrange("p a f -> p (a f)"),
                                start=s, stop=f, skip_group_check=True)

            def mul(tiles):
                def run(e, exact):
                    cg = regs["cg"]
                    if exact:
                        if tiles[0] == 0:
                            for g in range(NG):
                                e.wait_ge(*zm[g])
                        for c in tiles:
                            n = NT * p + c
                            if n >= 4:
                                e.wait_ge(s_pr, n - 3)
                            product(e, n, zb[:, :], 0, True, False)
                            with e.Fori(0, PL):
                                hold(e, (s_gl, cg))
                                e.reg_add(cg, cg, 16)
                                with e.Fori(0, NT - 1) as i:
                                    e.matmul(bank[n % 4][:, 0:3 * D], gslot[:, bass.ds(i * P, P)],
                                             z[:, bass.ds(i, 1), :, :].rearrange("p t a f -> p (t a f)"),
                                             start=False, stop=False, skip_group_check=True)
                                product(e, n, gslot[:, (NT - 1) * P:NT * P], NT - 1, False, False).then_inc(s_gd, 1)
                            product(e, n, zb[:, :], 0, False, True).then_inc(s_fr, 1)
                        return
                    sets = [tiles] if tiles[0] == 0 else [[c] for c in tiles]
                    for some in sets:
                        for c in some:
                            n = NT * p + c
                            if n >= 4:
                                e.wait_ge(s_pr, n - 3)
                            e.wait_ge(s_a[n % NSLOT], 16 * (n // NSLOT + 1))
                        for g in range(NG):
                            if tiles[0] == 0:
                                e.wait_ge(*zm[g])
                            for c in some:
                                n = NT * p + c
                                for i in range(g * GT, (g + 1) * GT):
                                    ins = product(e, n, slot[n % NSLOT][:, i * P:(i + 1) * P], i, i == 0, i == NT - 1)
                                if g == NG - 1:
                                    ins.then_inc(s_fr, 1)
                return run

            def add(n, c):
                def run(e, exact):
                    e.wait_ge(s_fr, n + 1)
                    e.tensor_reduce(A[:, c, :], bank[n % 4][:, 0:3 * D].rearrange("p (a f) -> p f a", a=3), AX.X, ALU.add) \
                        .then_inc(s_pr, 1)
                return run

            L.raw("s", load)
            got, m1 = {}, {}
            for g in range(NG):
                L.raw("t", mul(list(range(g * GT, g * GT + 4))))
                if proj and g:
                    proj.turn(g - 1, m1[g - 1])
                L.raw("t", mul(list(range(g * GT + 4, (g + 1) * GT))))
                free = before(g) if before else ()
                for c in range(g * GT, (g + 1) * GT):
                    L.raw("v", add(NT * p + c, c), *free)
                m1[g] = ready(g, (s_pr, NT * p + (g + 1) * GT))
                if proj and g:
                    got[g - 1] = proj.late(g - 1)
                if extra and g in extra:
                    extra[g]()
            if proj:
                proj.turn(NG - 1, m1[NG - 1])
                got[NG - 1] = proj.late(NG - 1)
                return got
            return m1

        def norm0(g, y, *w):
            s, m = gs(st[:, 0, :], g), gs(st[:, 1, :], g)
            k = red(s, y, ALU.add, *w)
            k = ts(m, s, 1.0 / D, None, ALU.mult, None, k)
            k = tt(gr(T, g), y, nb(st[:, 1, :], g), ALU.subtract, k)
            return act(gr(U, g), gr(T, g), ACT.Square, k)

        def norm1(g, *w):
            q = gs(st[:, 2, :], g)
            k = red(q, gr(U, g), ALU.add, *w)
            k = ts(q, q, 1.0 / D, EPS, ALU.mult, ALU.add, k)
            return act(gs(st[:, 0, :], g), q, ACT.Sqrt, k)

        def norm2(g, dst, *w):
            k = v(lambda e: e.reciprocal(gs(st[:, 3, :], g), gs(st[:, 0, :], g)), *w)
            return tt(dst, gr(T, g), nb(st[:, 3, :], g), ALU.mult, k)

        def part(src, g, *w):
            n = GT if g < NG - 1 else GT - 1
            return red(cs[:, g, :], src[:, g * GT:g * GT + n, :].rearrange("p t f -> p f t"), ALU.add, *w)

        def total(o, src, g, *w):
            k = t(lambda e: e.matmul(o, ones[:, :], cs[:, g, :], start=(g == 0), stop=False), *w)
            if g == NG - 1:
                k = t(lambda e: e.matmul(o, M[:, :], src[:, NT - 1, :], start=False, stop=True))
            return k

        one = v(lambda e: e.memset(ones[:, :], 1.0))
        v(lambda e: e.memset(zb[:, :], 0.0))
        k = v(lambda e: e.tensor_copy(cnt[:, :], S[:, :, D]))
        kd = ts(dv1[:, :], cnt[:, :], 1.0, None, ALU.add, None, k)
        ke = ts(dv2[:, :], cnt[:, :], 1e-12, None, ALU.max, None, k)
        k = ts(st[:, 2, :], cnt[:, :], 1.0, None, ALU.max, None, k)
        ki = v(lambda e: e.reciprocal(inv[:, :], st[:, 2, :]), k)
        kd = rsqrt(dv1[:, :], dv1[:, :], st[:, 0, :], kd)
        ke = rsqrt(dv2[:, :], dv2[:, :], st[:, 1, :], ke)
        k = t(lambda e: e.transpose(bank[7][:, 0:D], w0[:, :], ident[0:D, 0:D]), w0l)
        kw = v(lambda e: e.tensor_copy(w0t[:, :], bank[7][:, 0:D]), k)

        def l0_use(g, o, k):
            k = tt(gr(Y, g), o, gr(A, g), ALU.add, k, kb0[g])
            return k, k

        pj0 = Project(TU, 2 * D, w0t[:, :], l0_use, kw)
        kh, kb0, kx0 = {}, {}, {}
        for g in range(NG):
            kx0[g] = act(gr(T, g), gr(X, g), ACT.Copy)
        for g in range(NG):
            kh[g] = tt(gr(U, g), gr(S[:, :, 0:D], g), nb(inv, g), ALU.mult, ki, eng="g")
            kb0[g] = tt(gr(A, g), gr(X, g), fb(row["L0_gnn_b"][:, :]), ALU.add, w0l, eng="g")

        def l0(g, _):
            if g == 0:
                pj0.turn(0, kh[0], kx0[0])
            if g < NG - 1:
                pj0.turn(g + 1, kh[g + 1], kx0[g + 1])
            return pj0.late(g)

        z = 0
        zm = pipe(l0,
                  lambda g, k: norm0(g, gr(Y, g), k),
                  lambda g, k: norm1(g, k),
                  lambda g, k: norm2(g, gr(X, g), k),
                  lambda g, k: tt(gr(Y, g), gr(X, g), nb(dv1, g), ALU.mult, k, kd, eng="g"),
                  lambda g, k: split0(Z[0], g, gr(Y, g), k),
                  lambda g, k: split1(Z[0], g, gr(Y, g), k),
                  lambda g, k: split2(Z[0], g, k))
        first = tuple(kh.values())

        for i in range(3):
            def ready(g, k):
                k = tt(gr(A, g), gr(A, g), gr(Y, g), ALU.add, k)
                return tt(gr(A, g), gr(A, g), nb(dv1, g), ALU.mult, k)

            def use(g, o, k, i=i):
                k = tt(gr(R, g), o, fb(row[f"L1_gnn_b{i}"][:, :]), ALU.add, k)
                kc[g] = part(R, g, k)
                if g:
                    total(bank[7][:, 0:D], R, g - 1, kc[g - 1], one)
                if g == NG - 1:
                    kc["m"] = total(bank[7][:, 0:D], R, g, kc[g])
                return k, k

            kc = {}
            sweep(Z[z], zm, False, ready, Project(A, D, wmat[f"L1_gnn_W{i}"][:, :], use, wl), start=first)
            z = 1 - z
            kb = ts(bst[:, 0, :], bank[7][:, 0:D], 1.0 / N, None, ALU.mult, None, kc["m"])
            kq = {}

            def centre(g, _):
                kq[g] = tt(gr(T, g), gr(R, g), fb(bst[:, 0, :]), ALU.subtract, kb)
                return act(gr(U, g), gr(T, g), ACT.Square, kq[g])

            k = pipe(centre, lambda g, k: part(U, g, k), lambda g, k: total(bank[5][:, 0:D], U, g, k))[NG - 1]
            k = ts(bst[:, 1, :], bank[5][:, 0:D], 1.0 / N, EPS, ALU.mult, ALU.add, k)
            k = rsqrt(bst[:, 2, :], bst[:, 1, :], bst[:, 0, :], k)
            ks = tt(bst[:, 3, :], bst[:, 2, :], row[f"L1_gnn_gamma{i}"][:, :], ALU.mult, k, wl)

            def affine(g, _, i=i):
                k = tt(gr(T, g), gr(T, g), fb(bst[:, 3, :]), ALU.mult, ks, eng="g")
                return tt(gr(T, g), gr(T, g), fb(row[f"L1_gnn_beta{i}"][:, :]), ALU.add, k, wl, eng="g")

            def expo(g, k):
                k2 = act(gr(U, g), gr(T, g), ACT.Relu, k, scale=-1.0)
                return act(gr(U, g), gr(U, g), ACT.Exp, k2, scale=-1.0)

            def elu(g, k):
                k = ts(gr(T, g), gr(T, g), 0.0, -1.0, ALU.max, ALU.add, k)
                return tt(gr(R, g), gr(T, g), gr(U, g), ALU.add, k)

            if i < 2:
                zm = pipe(affine, expo, elu,
                          lambda g, k: tt(gr(Y, g), gr(R, g), nb(dv1, g), ALU.mult, k),
                          lambda g, k: split0(Z[z], g, gr(Y, g), k),
                          lambda g, k: split1(Z[z], g, gr(Y, g), k),
                          lambda g, k: split2(Z[z], g, k))
            else:
                kx = {}

                def last(g, k):
                    kx[g] = norm2(g, gr(X, g), k)
                    return tt(gr(Y, g), gr(X, g), nb(dv2, g), ALU.mult, kx[g], ke, eng="g")

                kn = pipe(affine, expo, elu,
                          lambda g, k: tt(gr(Y, g), gr(X, g), gr(R, g), ALU.add, k, eng="g"),
                          lambda g, k: norm0(g, gr(Y, g), k))
                zm = pipe(lambda g, _: norm1(g, kn[g]),
                          last,
                          lambda g, k: split0(Z[z], g, gr(Y, g), k),
                          lambda g, k: split1(Z[z], g, gr(Y, g), k),
                          lambda g, k: split2(Z[z], g, k))

        K = {}

        def stats0():
            for g in range(NG):
                k = total(bank[7][:, 0:D], X, g, part(X, g, kx[g]), one)
            for g in range(NG):
                t(lambda e, g=g: e.matmul(bank[6][0:D, 0:1], cs[:, g, :], ones[:, 0:1], start=(g == 0), stop=False))
            k2 = t(lambda e: e.matmul(bank[6][0:D, 0:1], X[:, NT - 1, :], M[:, 0:1], start=False, stop=True))
            K["xm"] = ts(xm[:, :], bank[6][0:D, 0:1], 1.0 / N, None, ALU.mult, None, k2)
            k = red(sc[:, 4:5], bank[7][:, 0:D], ALU.add, k)
            k = ts(sc[:, 0:1], sc[:, 4:5], 1.0 / (N * D), None, ALU.mult, None, k)
            K["u"] = {}
            for g in range(NG):
                k2 = ts(gr(U, g), gr(X, g), sc[:, 0:1], None, ALU.subtract, None, k)
                K["u"][g] = act(gr(U, g), gr(U, g), ACT.Square, k2)

        def stats1():
            for g in range(NG):
                k = total(bank[5][:, 0:D], U, g, part(U, g, K["u"][g], K["xm"]))
            k = red(sc[:, 5:6], bank[5][:, 0:D], ALU.add, k)
            k = ts(sc[:, 6:7], sc[:, 5:6], 1.0 / (N * D - 1), None, ALU.mult, None, k)
            k = act(sc[:, 1:2], sc[:, 6:7], ACT.Sqrt, k)
            v(lambda e: e.memset(sc[:, 2:3], float(N)))
            k3 = v(lambda e: e.memset(sc[:, 3:4], float(NE)))
            o = bank[4]
            kt = t(lambda e: e.transpose(o[0:D, 0:32], p1[:, 0:D], ident[0:32, 0:32]), wl)
            kt = t(lambda e: e.transpose(o[0:32, 64:70], p2[:, :], ident[0:6, 0:6]))
            kq = v(lambda e: e.tensor_copy(p1t[:, :], o[0:D, 0:32]), kt)
            kq = v(lambda e: e.tensor_copy(p2t[:, :], o[0:32, 64:70]))
            kt = t(lambda e: e.matmul(bank[7][0:32, 80:81], p1t[:, :], xm[:, :], start=True, stop=True), kq, K["xm"], k)
            k = tt(hh[:, 0:4], p1[:, D:D + 4], sc[0:32, 0:4], ALU.mult, k, k3, wl)
            k = red(hh[:, 4:5], hh[:, 0:4], ALU.add, k)
            k = tt(hh[:, 5:6], hh[:, 4:5], pb1[:, :], ALU.add, k)
            k = tt(hh[:, 6:7], hh[:, 5:6], bank[7][0:32, 80:81], ALU.add, k, kt)
            k = ts(hh[:, 7:8], hh[:, 6:7], 0.0, None, ALU.max, None, k)
            k = ts(hb[:, :], ones[0:32, :], hh[:, 7:8], None, ALU.mult, None, k)
            k = t(lambda e: e.matmul(bank[6][:, 96:102], hb[:, :], p2t[:, :], start=True, stop=True), k)
            k = tt(co[:, 0, :], bank[6][:, 96:102], pb2[:, :], ALU.add, k)
            k = red(sc[:, 8:9], co[:, 0, :], ALU.max, k)
            k = ts(co[:, 1, :], co[:, 0, :], sc[:, 8:9], None, ALU.subtract, None, k)
            k = act(co[:, 1, :], co[:, 1, :], ACT.Exp, k)
            k = red(sc[:, 9:10], co[:, 1, :], ALU.add, k)
            k = v(lambda e: e.reciprocal(sc[:, 10:11], sc[:, 9:10]), k)
            K["co"] = ts(co[:, 2, :], co[:, 1, :], sc[:, 10:11], None, ALU.mult, None, k)

        ka, kr = {}, {}

        def term(i, g):
            kr[g] = stt(gr(R, g), gr(A, g), co[:, 2, i:i + 1], gr(R, g), ALU.mult, ALU.add, ka[g], kr[g])

        for i in range(1, 6):
            nz = Z[1 - z]

            def before(g, i=i):
                if i == 2:
                    kr[g] = ts(gr(R, g), gr(X, g), co[:, 2, 0:1], None, ALU.mult, None, K["co"])
                if i >= 2:
                    term(i - 1, g)
                    return (kr[g],)
                return ()

            def ready(g, k, i=i, nz=nz):
                ka[g] = tt(gr(A, g), gr(A, g), nb(dv2, g), ALU.mult, k)
                if i < 5:
                    k = tt(gr(Y, g), gr(A, g), nb(dv2, g), ALU.mult, ka[g])
                    return split(nz, g, gr(Y, g), k)
                term(5, g)
                k = tt(gr(Y, g), gr(X, g), gr(R, g), ALU.add, kr[g])
                k = norm2(g, gr(X, g), norm1(g, norm0(g, gr(Y, g), k)))
                return split(nz, g, gr(X, g), k)

            zm = sweep(Z[z], zm, True, ready, before=before, extra={0: stats0, 1: stats1} if i == 1 else None)
            z = 1 - z

        def hidden(g, o, k):
            ko = tt(gr(R, g), o, fb(row["L3_gnn_b1"][:, :]), ALU.add, k)
            k = ts(gr(R, g), gr(R, g), 0.0, None, ALU.max, None, ko)
            return ko, split(Z[1 - z], g, gr(R, g), k)

        zm = sweep(Z[z], zm, False, lambda g, k: k, Project(A, D, wmat["L3_gnn_W1"][:, :], hidden, wl))
        z = 1 - z

        def final(g, o, k):
            ko = tt(gr(R, g), o, fb(row["L3_gnn_b2"][:, :]), ALU.add, k)
            k = tt(gr(Y, g), gr(X, g), gr(R, g), ALU.add, ko)
            k = norm2(g, gr(X, g), norm1(g, norm0(g, gr(Y, g), k)))
            c0, c1 = g * GT, min((g + 1) * GT, NT - 1)
            L.raw("s", lambda e, x: e.dma_start(out[c0 * P:c1 * P, :].rearrange("(t p) f -> p t f", p=P), X[:, c0:c1, :])
                  .then_inc(s_out, 16), k)
            if g == NG - 1:
                L.raw("s", lambda e, x: e.dma_start(out[(NT - 1) * P:N, :], X[0:LAST, NT - 1, :]).then_inc(s_out, 16))
            return ko, k

        sweep(Z[z], zm, False, lambda g, k: k, Project(A, D, wmat["L3_gnn_W2"][:, :], final, wl))
        L.raw("s", lambda e, x: e.wait_ge(s_out, 16 * (NG + 1)))
        L.raw("s", lambda e, x: e.wait_ge(*wl))

        b = C.enter_context(nc.Block())

        def both(name, e):
            go = values(nc, e, flag[0:1, 0:1])[0]
            with e.If(go < 1):
                L.run(name, e, False)
            with e.If(go > 0):
                L.run(name, e, True)

        @b.sync
        def _(e):
            regs["cd"] = e.alloc_register("s_cd")
            e.reg_mov(regs["cd"], 1)
            e.sem_inc(s_gd, 1)
            both("s", e)

        @b.gpsimd
        def _(e):
            both("g", e)

        @b.scalar
        def _(e):
            both("a", e)

        @b.tensor
        def _(e):
            regs["cg"] = e.alloc_register("t_cg")
            e.reg_mov(regs["cg"], 16)
            both("t", e)

        @b.vector
        def _(e):
            both("v", e)


_WEIGHTS = ["L0_gnn_W", "L0_gnn_b"] + [f"L1_gnn_{k}{i}" for i in range(3) for k in ("W", "b", "gamma", "beta")] + \
    [f"L{j}_gnn_{k}{i}" for j in (2, 3) for i in (1, 2) for k in ("W", "b")]


def kernel(**inputs):
    import numpy as _np
    import concourse.bacc as _bacc
    from concourse import mybir as _mybir
    from concourse.bass_utils import run_bass_kernel_spmd as _run

    def padded(a, n, fill):
        a = _np.asarray(a)
        return _np.concatenate([a, _np.full((n - a.shape[0],) + a.shape[1:], fill, a.dtype)])

    laid = {
        "x": padded(inputs["x"], NP_, 0),
        "src": padded(inputs["src"], NB * 512, 0).reshape(NB, 512),
        "dst": padded(inputs["dst"], NB * 512, 8191).reshape(NB, 512),
        "e": padded(inputs["edge_attr_64"], NB * 512, 0).reshape(NB, P, 4 * D),
    }
    for n in _WEIGHTS:
        laid[n] = _np.ascontiguousarray(inputs[n])
    nc = _bacc.Bacc("TRN2", target_bir_lowering=False, num_devices=1)
    arrays, args = {}, {}
    for n, v in laid.items():
        arrays[f"in_{n}"] = v
        args[n] = nc.dram_tensor(f"in_{n}", v.shape, _mybir.dt.from_np(v.dtype), kind="ExternalInput").ap()
    out = nc.dram_tensor("out_0", (N, D), F32, kind="ExternalOutput").ap()
    build(nc, args, out)
    r = _run(nc, [arrays], core_ids=[0])
    return r.results[0]["out_0"]
```
